# Optimizing a Trainium2 kernel written in Bass

```python
import numpy as np
import jax
import jax.numpy as jnp

def _softmax(x, axis=-1):
    return jax.nn.softmax(x, axis=axis)

def _gelu(x):
    return jax.nn.gelu(x, approximate=True)

def _silu(x):
    return jax.nn.silu(x)

def _sigmoid(x):
    return jax.nn.sigmoid(x)

def _layernorm(x, axis=-1, eps=1e-05):
    m = jnp.mean(x, axis=axis, keepdims=True)
    v = jnp.var(x, axis=axis, keepdims=True)
    return (x - m) / jnp.sqrt(v + eps)

def _scatter_add(tgt, idx, src, axis=0):
    return tgt.at[idx].add(src)

def _segment_sum(src, seg, n):
    return jax.ops.segment_sum(src, seg, n)
kernel_name = 'mk_adj_preln_d2_adj_r2_4b70e5'

def setup_inputs(seed: int=0):
    np.random.seed(seed)
    _w = jnp.asarray

    def _rec_inputs():
        import jax
        import jax.numpy as jnp
        _gk = jax.random.key(seed)
        x = -0.0002928 + 1 * jax.random.normal(jax.random.fold_in(_gk, 1), (4096, 256), jnp.float32)
        _a = jax.random.bernoulli(jax.random.fold_in(_gk, 2), 0.00390625, (4096, 4096))
        _a = jnp.logical_or(_a, jnp.swapaxes(_a, -1, -2))
        _a = jnp.logical_or(_a, jnp.eye(4096, dtype=bool))
        adj = _a
        return (x, adj)
    x, adj = _rec_inputs()

    def _L0_gnn_setup():
        import jax, jax.numpy as jnp
        import numpy as np
        N = 4096
        D_IN = 256
        D_HID = 512
        D_OUT = 256
        N_NEIGHS = 16
        key = jax.random.key(seed)
        k1, k2, k3 = jax.random.split(key, 3)
        x = jax.random.normal(k1, (N, D_IN), dtype=jnp.float32)
        rows = jnp.arange(N)[:, None]
        cols = (rows + 1 + jnp.arange(N_NEIGHS)[None, :]) % N
        fake_edge_mask = jnp.zeros((N, N), dtype=jnp.bool_).at[rows, cols].set(True)
        real_edge_mask = jnp.zeros((N, N), dtype=jnp.bool_)
        W1 = jax.random.normal(k2, (D_IN, D_HID), dtype=jnp.float32) * (1.0 / np.sqrt(D_IN))
        b1 = jnp.zeros((D_HID,), dtype=jnp.float32)
        W2 = jax.random.normal(k3, (D_HID, D_OUT), dtype=jnp.float32) * (1.0 / np.sqrt(D_HID))
        b2 = jnp.zeros((D_OUT,), dtype=jnp.float32)
        return {'x': x, 'real_edge_mask': real_edge_mask, 'fake_edge_mask': fake_edge_mask, 'W1': W1, 'b1': b1, 'W2': W2, 'b2': b2}
    _L0_gnn_all = _L0_gnn_setup()
    _L0_gnn_in = {k: v for k, v in _L0_gnn_all.items() if k in ('W1', 'b1', 'W2', 'b2')}
    del _L0_gnn_all

    def _L1_gnn_setup():
        import jax, jax.numpy as jnp
        import numpy as np
        N = 4096
        D = 256
        NEG = -1e+30
        key = jax.random.key(seed)
        ks = jax.random.split(key, 5)
        neuron_states = jax.random.normal(ks[0], (N, D), dtype=jnp.float32)
        adjacency = jax.random.bernoulli(ks[1], 0.05, (N, N))
        Wq = jax.random.normal(ks[2], (D, D), dtype=jnp.float32) / np.sqrt(D)
        Wk = jax.random.normal(ks[3], (D, D), dtype=jnp.float32) / np.sqrt(D)
        Wv = jax.random.normal(ks[4], (D, D), dtype=jnp.float32) / np.sqrt(D)
        return {'neuron_states': neuron_states, 'adjacency': adjacency, 'Wq': Wq, 'Wk': Wk, 'Wv': Wv}
    _L1_gnn_all = _L1_gnn_setup()
    _L1_gnn_in = {k: v for k, v in _L1_gnn_all.items() if k in ('Wq', 'Wk', 'Wv')}
    del _L1_gnn_all
    return {'x': x, 'adj': adj, 'L0_gnn_W1': _L0_gnn_in['W1'], 'L0_gnn_b1': _L0_gnn_in['b1'], 'L0_gnn_W2': _L0_gnn_in['W2'], 'L0_gnn_b2': _L0_gnn_in['b2'], 'L1_gnn_Wq': _L1_gnn_in['Wq'], 'L1_gnn_Wk': _L1_gnn_in['Wk'], 'L1_gnn_Wv': _L1_gnn_in['Wv']}

def reference(x, adj, L0_gnn_W1, L0_gnn_b1, L0_gnn_W2, L0_gnn_b2, L1_gnn_Wq, L1_gnn_Wk, L1_gnn_Wv):
    import jax
    import jax.numpy as jnp

    def _L0_gnn_ref(x, real_edge_mask, fake_edge_mask, W1, b1, W2, b2):
        import jax, jax.numpy as jnp
        import numpy as np
        N = 4096
        D_IN = 256
        D_HID = 512
        D_OUT = 256
        N_NEIGHS = 16
        _, idx = jax.lax.top_k(fake_edge_mask.astype(jnp.float32), N_NEIGHS)
        niche_feat = x[idx]
        res = jnp.sum(niche_feat, axis=1) / N_NEIGHS
        hidden = x + res
        h = jax.nn.relu(hidden @ W1 + b1)
        out = h @ W2 + b2
        return out

    def _L1_gnn_ref(neuron_states, adjacency, Wq, Wk, Wv):
        import jax, jax.numpy as jnp
        import numpy as np
        N = 4096
        D = 256
        NEG = -1e+30
        q = neuron_states @ Wq.T
        k = neuron_states @ Wk.T
        v = neuron_states @ Wv.T
        mask = adjacency.T
        scores = jnp.where(mask, q @ k.T, NEG)
        attn = jax.nn.softmax(scores, axis=1)
        attn = jnp.where(mask, attn, 0.0)
        return attn @ v
    h = jnp.maximum(_layernorm(x, axis=-1), 0.0)
    x = x + _L0_gnn_ref(h, adj, adj, L0_gnn_W1, L0_gnn_b1, L0_gnn_W2, L0_gnn_b2)
    h = jnp.maximum(_layernorm(x, axis=-1), 0.0)
    x = x + _L1_gnn_ref(h, adj, L1_gnn_Wq, L1_gnn_Wk, L1_gnn_Wv)
    return x

_drawn_inputs = setup_inputs


def setup_inputs(seed=0):
    import zlib

    import numpy as np

    out = dict(_drawn_inputs(seed))
    spreads = {'L0_gnn_b1': (0.0, 0.1), 'L0_gnn_b2': (0.0, 0.1)}
    factors = {}
    for name, (base, spread) in spreads.items():
        noise = np.random.default_rng([zlib.crc32(name.encode()), seed]).standard_normal(out[name].shape)
        drawn = base * np.exp(spread * noise) if base else spread * noise
        out[name] = jnp.asarray(drawn.astype(out[name].dtype))
    for name, factor in factors.items():
        out[name] = (out[name] * factor).astype(out[name].dtype)
    return out
```

```python
import math
from contextlib import ExitStack
import concourse.bass as bass
from concourse import mybir

F32, F16, U8 = mybir.dt.float32, mybir.dt.float16, mybir.dt.uint8
I32, U32 = mybir.dt.int32, mybir.dt.uint32
ALU, ACT, AX = mybir.AluOpType, mybir.ActivationFunctionType, mybir.AxisListType

P = 128
N, D, HID = 4096, 256, 512
CH = 512
NC = N // CH
KT = N // P
TC = CH // P
DH = D // P
HB = HID // P
GR = 4
GW = N // GR
NW = GW // 128
NEIGH = 16
PAIRS = N // 2
EPS = 1e-5
SCAN_AT = [2, 5, 7, 16]
H_SCALE = 2048.0
P_SCALE = 16384.0
NEG = -1.0e30
NEG_FLOOR = -5.0e29
TINY = 1e-30
ST_RING, X_RING, QK_RING = 8, 8, 2
LAG = 5
V_W = D + 2


class Chain:

    def __init__(self, engine, sem, per):
        self.engine, self.sem, self.per = engine, sem, per

    def begin(self, chunk):
        self.chunk, self.n = chunk, 0

    def then(self, instruction):
        instruction.then_inc(self.sem, 1)
        self.n += 1
        self.engine.wait_ge(self.sem, self.chunk * self.per + self.n)

    def end(self):
        assert self.n == self.per, (self.n, self.per)


def build(nc, x, adj, w1, b1, w2, b2, wq, wk, wv, out):
    x2_dram = nc.dram_tensor("x2_scratch", (N, D), F32, kind="Internal").ap()
    h_dram = nc.dram_tensor("h_scratch", (N, 2 * D), F16, kind="Internal").ap()
    with ExitStack() as ctx:
        def sb(name, shape, dt):
            return ctx.enter_context(nc.sbuf_tensor(name, shape, dt))

        keep = {}
        keep["h2t"] = sb("h2t", [P, DH, 2, N], F16)
        keep["v_hi"] = sb("v_hi", [P, KT, V_W], F16)
        keep["v_lo"] = sb("v_lo", [P, KT, D], F16)
        keep["ident"] = sb("ident", [P, P], F32)
        keep["ones"] = sb("ones", [P, P], F32)
        keep["ident16"] = sb("ident16", [P, P], F16)
        keep["a_sp"] = sb("a_sp", [P, DH, 2, D], F16)
        keep["exp_scale"] = sb("exp_scale", [P, 1], F32)
        keep["wvt"] = sb("wvt", [P, DH, D], F32)
        setup(nc, x, wq, wk, wv, h_dram, keep)
        layer0(nc, x, adj, w1, b1, w2, b2, h_dram, x2_dram, keep)
        layer1(nc, adj, x2_dram, out, keep)


def group_rows(t, w):
    return [t[g * GW + w * P:g * GW + (w + 1) * P, :].rearrange("(r b) m -> r (b m)", b=4)
            for g in range(GR)]


def setup(nc, x, wq, wk, wv, h_dram, keep):
    with ExitStack() as ctx:
        def sb(name, shape, dt):
            return ctx.enter_context(nc.sbuf_tensor(name, shape, dt))

        def pb(name, shape, dt):
            return ctx.enter_context(nc.psum_tensor(name, shape, dt))

        def sem(name):
            return ctx.enter_context(nc.semaphore(name))

        ident, ones, ident16 = keep["ident"], keep["ones"], keep["ident16"]
        a_sp, exp_scale, wvt, v_hi = keep["a_sp"], keep["exp_scale"], keep["wvt"], keep["v_hi"]
        wq_sb = sb("wq_sb", [P, DH, D], F32)
        wk_sb = sb("wk_sb", [P, DH, D], F32)
        wv_sb = sb("wv_sb", [P, DH, D], F32)
        a_f = sb("a_f", [P, DH, D], F32)
        a_abs = sb("a_abs", [P, 4], F32)
        a_row = sb("a_row", [1, P], F32)
        sc = sb("sc", [1, 8], F32)
        a_ps = pb("a_ps", [P, DH, D], F32)
        v_ps = pb("v_ps", [P, DH, D], F32)
        m_ps = pb("m_ps", [P, P + 1], F32)
        w_loaded, consts, zeroed = sem("w_loaded"), sem("s_consts"), sem("s_zeroed")
        a_done, wvt_done, row_done, bc_done = sem("a_done"), sem("wvt_done"), sem("row_done"), sem("bc_done")
        max_ready, scale_ready, dve_chain = sem("max_ready"), sem("scale_ready"), sem("setup_chain")
        block = ctx.enter_context(nc.Block())

        @block.sync
        def _(sp):
            for dst, src in ((wq_sb, wq), (wk_sb, wk), (wv_sb, wv)):
                sp.dma_start(dst[:, :, :], src.rearrange("(o p) d -> p o d", p=P)).then_inc(w_loaded, 16)

        @block.gpsimd
        def _(pool):
            nc.gpsimd.memset(ident[:, :], 0.0).then_inc(zeroed, 1)
            nc.gpsimd.memset(ident16[:, :], 0.0).then_inc(zeroed, 1)
            nc.gpsimd.memset(ones[:, :], 1.0).then_inc(consts, 1)
            nc.gpsimd.memset(v_hi[:, :, D:V_W], 1.0).then_inc(consts, 1)
            pool.wait_ge(zeroed, 2)
            for m in (ident, ident16):
                nc.gpsimd.affine_select(out=m[:, :], in_=m[:, :], compare_op=ALU.not_equal, fill=1.0,
                                        base=0, pattern=[[-1, P]], channel_multiplier=1).then_inc(consts, 1)

        @block.tensor
        def _(pe):
            pe.wait_ge(w_loaded, 48)
            for h in range(DH):
                for o in range(DH):
                    last = nc.tensor.matmul(a_ps[:, h, :], wq_sb[:, o, h * P:(h + 1) * P], wk_sb[:, o, :],
                                            start=(o == 0), stop=(o == DH - 1))
            last.then_inc(a_done, 1)
            pe.wait_ge(consts, 4)
            for h in range(DH):
                for o in range(DH):
                    last = nc.tensor.transpose(v_ps[:, h, o * P:(o + 1) * P],
                                               wv_sb[:, o, h * P:(h + 1) * P], ident[:, :])
            last.then_inc(wvt_done, 1)
            pe.wait_ge(max_ready, 1)
            nc.tensor.transpose(m_ps[0:1, 0:P], a_abs[:, 0:1], ident[:, :]).then_inc(row_done, 1)
            pe.wait_ge(scale_ready, 1)
            nc.tensor.matmul(m_ps[:, P:P + 1], ones[0:1, :], sc[0:1, 2:3], start=True, stop=True).then_inc(bc_done, 1)

        @block.vector
        def _(dve):
            seq = Chain(dve, dve_chain, 10)
            seq.begin(0)
            dve.wait_ge(a_done, 1)
            seq.then(nc.vector.tensor_copy(a_f[:, :, :], a_ps[:, :, :]))
            seq.then(nc.vector.tensor_single_scalar(a_abs[:, 1:2], a_f[:, 0, 0:1], 0.0, ALU.mult))
            nc.vector.tensor_reduce(out=a_abs[:, 0:1], in_=a_f[:, :, :], axis=AX.XY, op=ALU.max,
                                    apply_absolute_value=True).then_inc(max_ready, 1)
            dve.wait_ge(row_done, 1)
            seq.then(nc.vector.tensor_reduce(out=sc[0:1, 0:1], in_=m_ps[0:1, 0:P], axis=AX.X, op=ALU.max))
            seq.then(nc.vector.tensor_scalar(sc[0:1, 0:1], sc[0:1, 0:1], 2.0 ** -40, 1.0 / 128, ALU.max, ALU.mult))
            seq.then(nc.vector.reciprocal(sc[0:1, 1:2], sc[0:1, 0:1]))
            nc.vector.tensor_single_scalar(sc[0:1, 2:3].bitcast(U32), sc[0:1, 1:2].bitcast(U32), 0x7F800000,
                                           ALU.bitwise_and).then_inc(scale_ready, 1)
            dve.wait_ge(bc_done, 1)
            seq.then(nc.vector.tensor_copy(a_abs[:, 2:3], m_ps[:, P:P + 1]))
            seq.then(nc.vector.tensor_single_scalar(a_abs[:, 3:4], a_abs[:, 2:3], H_SCALE, ALU.mult))
            seq.then(nc.vector.reciprocal(exp_scale[:, :], a_abs[:, 3:4]))
            seq.then(nc.vector.tensor_scalar(a_f[:, :, :], a_f[:, :, :], a_abs[:, 2:3], None, ALU.mult))
            seq.then(nc.vector.tensor_copy(a_sp[:, :, 0, :], a_f[:, :, :]))
            nc.vector.tensor_tensor(a_sp[:, :, 1, :], a_f[:, :, :], a_sp[:, :, 0, :], ALU.subtract)
            dve.wait_ge(wvt_done, 1)
            nc.vector.tensor_single_scalar(wvt[:, :, :], v_ps[:, :, :], 1.0 / H_SCALE, ALU.mult)
            seq.end()


def layer0(nc, x, adj, w1, b1, w2, b2, h_dram, x2_dram, keep):
    with ExitStack() as ctx:
        def sb(name, shape, dt):
            return ctx.enter_context(nc.sbuf_tensor(name, shape, dt))

        def pb(name, shape, dt):
            return ctx.enter_context(nc.psum_tensor(name, shape, dt))

        def sem(name):
            return ctx.enter_context(nc.semaphore(name))

        ident, ones, ident16 = keep["ident"], keep["ones"], keep["ident16"]
        h2t, v_hi, v_lo = keep["h2t"], keep["v_hi"], keep["v_lo"]
        w1_sb = sb("w1_sb", [P, DH, HID], F32)
        w2_sb = sb("w2_sb", [P, HB, D], F32)
        b1_sb = sb("b1_sb", [P, HB], F32)
        b2_sb = sb("b2_sb", [1, D], F32)
        h_j = sb("h_j", [P, KT, 2, D], F16)
        h_16 = sb("h_16", [NEIGH, 2, D], F16)
        h_nat = sb("h_nat", [P, TC, 2, D], F16)
        sixteen_i = sb("sixteen_i", [P, P], F16)
        j_col = sb("j_col", [P, KT], F32)
        j_int = sb("j_int", [P, KT], I32)
        half_col = sb("half_col", [P, 2], F32)
        adj_nat = sb("adj_nat", [P, 2, N], U8)
        adj_blk = sb("adj_blk", [P, CH // 32, GW], U8)
        adj_t = sb("adj_t", [P, NW, CH, 4], U8)
        cum = sb("cum", [P, 2, PAIRS], F16)
        sign_out = sb("sign_out", [P, PAIRS], mybir.dt.int8)
        acc = sb("acc", [P, TC, 2], F32)
        thr = sb("thr", [P, 3, TC], F32)
        fill_na = sb("fill_na", [P, NEIGH], F32)
        fill_rank = sb("fill_rank", [P, NEIGH], F32)
        fill_zero = sb("fill_zero", [P, NEIGH], F32)
        fill_need = sb("fill_need", [P, 1], F32)
        fill = sb("fill", [P, TC, NEIGH], F16)
        fill_t = sb("fill_t", [NEIGH, CH], F16)
        thr_diag = sb("thr_diag", [P, TC, P], F32)
        thr_b = sb("thr_b", [P, CH], F32)
        st = sb("st", [P, ST_RING, CH], F16)
        hid_t = sb("hid_t", [P, DH, CH], F32)
        act_t = sb("act_t", [P, HB, CH], F32)
        x_in = sb("x_in", [P, TC, D], F32)
        x2_sb = sb("x2_sb", [P, TC, D], F32)
        stats = sb("stats", [P, TC, 6], F32)
        mv = sb("mv", [P, TC, 2], F32)
        rs = sb("rs", [P, TC, 2], F32)
        var = sb("var", [P, TC], F32)
        wait_pad = sb("wait_pad", [P, 1], F32)
        std = sb("std", [P, TC], F32)
        inv = sb("inv", [P, TC, 2], F32)
        h32 = sb("h32", [P, TC, D], F32)
        h2_st = sb("h2_st", [P, 2, TC, D], F16)
        x_all = h2t[:, :, :, :].rearrange("p h s n -> p (h s n)").bitcast(F32).rearrange("p (k m) -> p k m", k=KT)
        scratch = v_lo[:, :, :].rearrange("p k m -> p (k m)").bitcast(F32)

        def part(at, width):
            return scratch[:, at * KT:(at + width) * KT].rearrange("p (t n) -> p t n", n=width)
        ln1_set = (part(0, 6), part(6, 2), part(8, 1)[:, :, 0], part(9, 1)[:, :, 0], part(10, 2), part(12, 2))
        ln2_set = (stats, mv, var[:, :], std[:, :], inv, rs)
        res_ps = pb("res_ps", [P, DH, CH], F32)
        hid_ps = pb("hid_ps", [P, 2, CH], F32)
        mlp_ps = pb("mlp_ps", [P, TC, D], F32)
        thr_ps = pb("thr_ps", [P, CH], F32)
        tr_ps = pb("tr_ps", [P, 2, CH], F16)
        w_loaded = sem("mlp_weights_loaded")
        col_loaded = [sem(f"x_col_loaded{w}") for w in range(NW)]
        consts = sem("l0_consts")
        pool_chain = sem("l0_pool_chain")
        h_scaled, h_hi_done, h_lo_done, h_stored = sem("h_scaled"), sem("h_hi_done"), sem("h_lo_done"), sem("h_stored")
        h_relu, h16_loaded, ln_ready = sem("h_relu"), sem("h16_loaded"), sem("ln_ready")
        ln1_chain, prep_chain, ln2_chain = sem("ln1_chain"), sem("prep_chain"), sem("ln2_chain")
        nat_loaded = [sem(f"nat_loaded{i}") for i in range(2)]
        blk_loaded, scanned, transposed, counted = sem("blk_loaded"), sem("scanned"), sem("transposed"), sem("counted")
        tile_read, diag_ready, fill_ready = sem("tile_read"), sem("diag_ready"), sem("fill_ready")
        thr_done, fill_tr_done, thr_copied, fill_copied = sem("thr_done"), sem("fill_tr_done"), sem("thr_copied"), sem("fill_copied")
        st_ready, st_used, hnat_loaded, res_done = sem("st_ready"), sem("st_used"), sem("hnat_loaded"), sem("res_done")
        hid_in_ready, hid_done, act_ready, mlp_done = sem("hid_in_ready"), sem("hid_done"), sem("act_ready"), sem("mlp_done")
        xin_loaded, x2_added, x2_stored = sem("xin_loaded"), sem("x2_added"), sem("x2_stored")
        std1_done, std2_done, var2_ready = sem("std1_done"), sem("std2_done"), sem("var2_ready")
        ln2_ready, h2_relu, h2_hi, h2_lo = sem("ln2_ready"), sem("h2_relu"), sem("h2_hi"), sem("h2_lo")
        h2_tr, h2_copied, v_stored = sem("h2_tr"), sem("h2_copied"), sem("v_stored")
        block = ctx.enter_context(nc.Block())

        def rows(t, c):
            return t[bass.ds(c * CH, CH), :].rearrange("(t p) m -> p t m", p=P)

        @block.sync
        def _(sp):
            def load_nat(c, t):
                n = c * TC + t
                if not (isinstance(c, int) and n < 2):
                    sp.wait_ge(scanned, n - 1)
                    sp.wait_ge(tile_read, n - 1)
                sp.dma_start(adj_nat[:, t % 2, :], adj[bass.ds(c * CH + t * P, P), :]).then_inc(nat_loaded[t % 2], 16)

            def load_blk(c):
                if not (isinstance(c, int) and c == 0):
                    sp.wait_ge(transposed, c)
                for g in range(GR):
                    src = adj[bass.ds(c * CH, CH), g * GW:(g + 1) * GW].rearrange("(i c) m -> c i m", c=32)
                    sp.dma_start(adj_blk[32 * g:32 * (g + 1), :, :], src).then_inc(blk_loaded, 16)

            load_nat(0, 0)
            load_nat(0, 1)
            for w in range(NW):
                for g, src in enumerate(group_rows(x, w)):
                    sp.dma_start(x_all[32 * g:32 * (g + 1), 4 * w:4 * (w + 1), :].rearrange("p b m -> p (b m)"), src)\
                        .then_inc(col_loaded[w], 16)
            load_nat(0, 2)
            load_nat(0, 3)
            load_blk(0)
            sp.dma_start(w1_sb[:, :, :], w1.rearrange("(o p) n -> p o n", p=P)).then_inc(w_loaded, 16)
            sp.dma_start(w2_sb[:, :, :], w2.rearrange("(o p) n -> p o n", p=P)).then_inc(w_loaded, 16)
            sp.dma_start(b1_sb[:, :], b1.rearrange("(o p) -> p o", p=P), allow_slow_non_contiguous=True).then_inc(w_loaded, 16)
            sp.dma_start(b2_sb[:, :], b2.rearrange("(a n) -> a n", a=1)).then_inc(w_loaded, 16)
            for w in range(NW):
                sp.wait_ge(h_hi_done, w + 1)
                sp.wait_ge(h_lo_done, w + 1)
                for g, dst in enumerate(group_rows(h_dram, w)):
                    sp.dma_start(dst, h_j[32 * g:32 * (g + 1), 4 * w:4 * (w + 1), :, :]
                                 .rearrange("p b s m -> p (b s m)")).then_inc(h_stored, 16)
            sp.wait_ge(h_stored, 16 * GR * NW)
            sp.dma_start(h_16[:, :, :], h_dram[0:NEIGH, :].rearrange("p (s m) -> p s m", s=2)).then_inc(h16_loaded, 16)
            load_nat(1, 0)
            load_nat(1, 1)
            load_blk(1)

            def chunk(c, first=False, more=True, more2=True):
                if not first:
                    sp.wait_ge(res_done, c)
                sp.dma_start(h_nat[:, :, :, :], h_dram[bass.ds(c * CH, CH), :]
                             .rearrange("(t p) (s m) -> p t s m", p=P, s=2)).then_inc(hnat_loaded, 16)
                if more:
                    load_nat(c + 1, 2)
                    load_nat(c + 1, 3)
                if more2:
                    load_nat(c + 2, 0)
                if not first:
                    finish_rows(c - 1)
                sp.dma_start(x_in[:, :, :], rows(x, c)).then_inc(xin_loaded, 16)
                if not first:
                    store_values(c - 1)
                if more2:
                    load_nat(c + 2, 1)
                    load_blk(c + 2)

            def finish_rows(c):
                sp.wait_ge(x2_added, c + 1)
                sp.dma_start(rows(x2_dram, c), x2_sb[:, :, :]).then_inc(x2_stored, 16)

            def store_values(c):
                sp.wait_ge(h2_hi, c + 1)
                sp.wait_ge(h2_lo, c + 1)
                sp.dma_start(v_hi[:, bass.ds(c * TC, TC), 0:D], h2_st[:, 0, :, :]).then_inc(v_stored, 16)
                sp.dma_start(v_lo[:, bass.ds(c * TC, TC), :], h2_st[:, 1, :, :]).then_inc(v_stored, 16)

            chunk(0, first=True)
            with sp.Fori(1, NC - 2) as c:
                chunk(c)
            chunk(NC - 2, more2=False)
            chunk(NC - 1, more=False, more2=False)
            finish_rows(NC - 1)
            store_values(NC - 1)
            sp.wait_ge(x2_stored, 16 * NC)
            sp.wait_ge(v_stored, 32 * NC)

        @block.gpsimd
        def _(pool):
            nc.gpsimd.iota(j_int[:, :], pattern=[[P, NW], [1, 4]], base=0, channel_multiplier=4).then_inc(consts, 1)
            nc.gpsimd.memset(half_col[:, 0:1], NEIGH - 0.5).then_inc(consts, 1)
            nc.gpsimd.memset(half_col[:, 1:2], NEIGH + 0.5).then_inc(consts, 1)
            nc.gpsimd.memset(fill_zero[:, :], 0.0).then_inc(consts, 1)
            nc.gpsimd.memset(sixteen_i[:, :], 0.0).then_inc(pool_chain, 1)
            pool.wait_ge(pool_chain, 1)
            nc.gpsimd.affine_select(out=sixteen_i[:, :], in_=sixteen_i[:, :], compare_op=ALU.not_equal,
                                    fill=float(NEIGH), base=0, pattern=[[-1, P]], channel_multiplier=1)\
                .then_inc(consts, 1)
            for w in range(NW):
                k = slice(4 * w, 4 * (w + 1))
                pool.wait_ge(h_hi_done, w + 1)
                nc.gpsimd.tensor_tensor(h_j[:, k, 1, :], x_all[:, k, :], h_j[:, k, 0, :], ALU.subtract)\
                    .then_inc(h_lo_done, 1)

            def ln2_low(c):
                pool.wait_ge(h2_hi, c + 1)
                if not (isinstance(c, int) and c == 0):
                    pool.wait_ge(v_stored, 32 * c)
                    pool.wait_ge(h2_tr, 2 * c)
                nc.gpsimd.tensor_tensor(h2_st[:, 1, :, :], h32[:, :, :], h2_st[:, 0, :, :], ALU.subtract)\
                    .then_inc(h2_lo, 1)

            ln2_low(0)
            with pool.Fori(1, NC) as c:
                ln2_low(c)

        @block.vector
        def _(dve):
            ln1 = Chain(dve, ln1_chain, 6)
            prep = Chain(dve, prep_chain, 4 * TC + 4)
            ln2 = Chain(dve, ln2_chain, 6)

            def row_var(src, chain, ready, at, tiles, arrived=None):
                stats, mv, var = at[0:3]
                for t in range(tiles):
                    if arrived and t % 4 == 0:
                        dve.wait_ge(arrived[t // 4], 16 * GR)
                    last = nc.vector.bn_stats(stats[:, t, :], src[:, t, :])
                chain.then(last)
                nc.vector.memset(wait_pad[:, :], 0.0)
                for t in range(tiles):
                    last = nc.vector.bn_aggr(mv[:, t, :], stats[:, t, :])
                chain.then(last)
                nc.vector.tensor_single_scalar(var, mv[:, :, 1], EPS, ALU.add).then_inc(ready, 1)

            def row_scale(chain, done, before, at):
                mv, var, std, inv, rs = at[1:]
                dve.wait_ge(done, before)
                chain.then(nc.vector.reciprocal(inv[:, :, 0], std))
                chain.then(nc.vector.tensor_tensor(inv[:, :, 1], inv[:, :, 0], inv[:, :, 0], ALU.mult))
                chain.then(nc.vector.scalar_tensor_tensor(inv[:, :, 1], inv[:, :, 1], -0.5 * H_SCALE, var,
                                                          ALU.mult, ALU.mult))
                chain.then(nc.vector.scalar_tensor_tensor(rs[:, :, 0], inv[:, :, 1], 1.5 * H_SCALE, inv[:, :, 0],
                                                          ALU.add, ALU.mult))
                return nc.vector.scalar_tensor_tensor(rs[:, :, 1], mv[:, :, 0], -1.0, rs[:, :, 0],
                                                      ALU.mult, ALU.mult)

            def scan_tile(c, t):
                n = c * TC + t
                dve.wait_ge(nat_loaded[t % 2], 16 * (c * 2 + t // 2 + 1))
                if not (isinstance(c, int) and n < 2):
                    dve.wait_ge(counted, 2 * (n - 1))
                if t == 0 and not (isinstance(c, int) and c == 0):
                    dve.wait_ge(fill_tr_done, c)
                pairs = adj_nat[:, t % 2, :].rearrange("p (n b) -> p n b", b=2)
                nc.vector.tensor_tensor_scan(cum[:, t % 2, :], pairs[:, :, 0], pairs[:, :, 1], 0.0,
                                             ALU.add, ALU.add).then_inc(scanned, 1)
                nc.vector.tensor_scalar(fill_na[:, :], adj_nat[:, t % 2, 0:NEIGH], -1.0, 1.0, ALU.mult, ALU.add)\
                    .then_inc(tile_read, 1)
                dve.wait_ge(tile_read, n + 1)
                prep.then(nc.vector.tensor_tensor_scan(fill_rank[:, :], fill_na[:, :], fill_zero[:, :], 0.0,
                                                       ALU.add, ALU.add))
                dve.wait_ge(scanned, n + 1)
                prep.then(nc.vector.tensor_scalar(fill_need[:, :], cum[:, t % 2, PAIRS - 1:PAIRS], -1.0,
                                                  float(NEIGH), ALU.mult, ALU.add))
                prep.then(nc.vector.scalar_tensor_tensor(fill[:, t, :], fill_rank[:, :], fill_need[:, :],
                                                         fill_na[:, :], ALU.is_le, ALU.mult))

            def transpose_chunk(c):
                dve.wait_ge(blk_loaded, 16 * GR * (c + 1))
                if not (isinstance(c, int) and c == 0):
                    dve.wait_ge(st_ready, KT * c)
                src = adj_blk[:, :, :].bitcast(U32)
                dst = adj_t[:, :, :, :].rearrange("p w i b -> p (w i b)").bitcast(U32)\
                    .rearrange("p (w i) -> p w i", w=NW)
                for i in range(CH // 32):
                    last = nc.vector.transpose(dst[:, :, 32 * i:32 * (i + 1)],
                                               src[:, i, :].rearrange("p (w r) -> p w r", w=NW))
                last.then_inc(transposed, 1)
                dve.wait_ge(transposed, c + 1)

            def thresholds(c):
                dve.wait_ge(counted, 2 * TC * (c + 1))
                prep.then(nc.vector.tensor_scalar(thr[:, 0:2, :].rearrange("p s t -> p t s"), acc[:, :, :],
                                                  float(PAIRS), 0.5, ALU.add, ALU.mult))
                prep.then(nc.vector.tensor_tensor(thr[:, 1, :], thr[:, 1, :], thr[:, 0, :], ALU.subtract))
                prep.then(nc.vector.tensor_single_scalar(thr[:, 1, :], thr[:, 1, :], 1.0, ALU.min))
                prep.then(nc.vector.scalar_tensor_tensor(thr[:, 2, :], thr[:, 0, :], 2.0, thr[:, 1, :],
                                                         ALU.mult, ALU.add))
                for t in range(TC):
                    prep.then(nc.vector.tensor_scalar(thr_diag[:, t, :], ident[:, :], thr[:, 2, t:t + 1], None,
                                                      ALU.mult))
                prep.end()

            def select_tile(c, k):
                if not (isinstance(c, int) and c == 0 and k < ST_RING):
                    dve.wait_ge(st_used, c * KT + k - ST_RING + 1)
                nc.vector.scalar_tensor_tensor(st[:, k % ST_RING, :], thr_b[:, :], j_col[:, k:k + 1],
                                               adj_t[:, k // 4, :, k % 4], ALU.is_ge, ALU.mult)\
                    .then_inc(st_ready, 1)

            def ln2_stats(c):
                ln2.begin(c)
                dve.wait_ge(mlp_done, c + 1)
                dve.wait_ge(xin_loaded, 16 * (c + 1))
                if not (isinstance(c, int) and c == 0):
                    dve.wait_ge(x2_stored, 16 * c)
                nc.vector.tensor_tensor(x2_sb[:, :, :], mlp_ps[:, :, :], x_in[:, :, :], ALU.add).then_inc(x2_added, 1)
                dve.wait_ge(x2_added, c + 1)
                if not (isinstance(c, int) and c == 0):
                    dve.wait_ge(h2_relu, TC * c)
                row_var(x2_sb, ln2, var2_ready, ln2_set, TC)

            def ln2_scale(c):
                row_scale(ln2, std2_done, c + 1, ln2_set).then_inc(ln2_ready, 1)
                ln2.end()

            dve.wait_ge(consts, 5)
            for g in range(GR):
                last = nc.vector.tensor_single_scalar(j_col[32 * g:32 * (g + 1), :], j_int[32 * g:32 * (g + 1), :],
                                                      float((GW - P) * g), ALU.add)
            last.then_inc(consts, 1)
            def chunk(c, first=False, more=True):
                if more:
                    prep.begin(c + 1)
                dve.wait_ge(thr_copied, c + 1)
                for k in range(KT):
                    select_tile(c, k)
                    if more and k in SCAN_AT:
                        scan_tile(c + 1, SCAN_AT.index(k))
                    if not first and k == 9:
                        ln2_stats(c - 1)
                    if not first and k == 12:
                        ln2_scale(c - 1)
                if more:
                    thresholds_and_signal(c + 1)
                    transpose_chunk(c + 1)

            def thresholds_and_signal(c):
                thresholds(c)
                nc.vector.sem_inc(diag_ready, 1)

            prep.begin(0)
            scan_tile(0, 0)
            scan_tile(0, 1)
            ln1.begin(0)
            row_var(x_all, ln1, ln_ready, ln1_set, KT, col_loaded)
            row_scale(ln1, std1_done, 1, ln1_set).then_inc(h_scaled, 1)
            ln1.end()
            scan_tile(0, 2)
            scan_tile(0, 3)
            for w in range(NW):
                dve.wait_ge(h_relu, 4 * (w + 1))
                nc.vector.tensor_copy(h_j[:, 4 * w:4 * (w + 1), 0, :], x_all[:, 4 * w:4 * (w + 1), :])\
                    .then_inc(h_hi_done, 1)
            thresholds_and_signal(0)
            transpose_chunk(0)
            chunk(0, first=True)
            with dve.Fori(1, NC - 1) as c:
                chunk(c)
            chunk(NC - 1, more=False)
            ln2_stats(NC - 1)
            ln2_scale(NC - 1)

        @block.scalar
        def _(act):
            def relu_rows(src, done):
                for t in range(TC):
                    nc.scalar.activation(h32[:, t, :], src[:, t, :], ACT.Relu, bias=rs[:, t, 1:2],
                                         scale=rs[:, t, 0:1]).then_inc(done, 1)

            def count_tile(c, t):
                act.wait_ge(scanned, c * TC + t + 1)
                if t == 0 and not (isinstance(c, int) and c == 0):
                    act.wait_ge(diag_ready, c)
                for s in range(2):
                    n = 2 * (c * TC + t) + s
                    if not (isinstance(c, int) and n == 0):
                        act.wait_ge(counted, n)
                    nc.scalar.activation(sign_out[:, :], cum[:, t % 2, :], ACT.Sign, bias=half_col[:, s:s + 1],
                                         scale=-1.0, accum_out=acc[:, t, s:s + 1]).then_inc(counted, 1)

            def copy_prep(c):
                act.wait_ge(thr_done, c + 1)
                nc.scalar.activation(thr_b[:, :], thr_ps[:, :], ACT.Copy).then_inc(thr_copied, 1)
                act.wait_ge(fill_tr_done, c + 1)
                nc.scalar.activation(fill_t[:, :], tr_ps[0:NEIGH, 0, :], ACT.Copy).then_inc(fill_copied, 1)

            def ln2_rows(c):
                act.wait_ge(var2_ready, c + 1)
                nc.scalar.activation(std[:, :], var[:, :], ACT.Sqrt).then_inc(std2_done, 1)
                act.wait_ge(ln2_ready, c + 1)
                if not (isinstance(c, int) and c == 0):
                    act.wait_ge(h2_lo, c)
                relu_rows(x2_sb, h2_relu)
                act.wait_ge(h2_relu, TC * (c + 1))
                if not (isinstance(c, int) and c == 0):
                    act.wait_ge(v_stored, 32 * c)
                    act.wait_ge(h2_tr, 2 * c)
                nc.scalar.activation(h2_st[:, 0, :, :], h32[:, :, :], ACT.Copy).then_inc(h2_hi, 1)

            def copy_h2t(c):
                for h in range(DH):
                    act.wait_ge(h2_tr, DH * c + h + 1)
                    nc.scalar.activation(h2t[:, h, :, bass.ds(c * CH, CH)], tr_ps[:, :, :], ACT.Copy)\
                        .then_inc(h2_copied, 1)

            def mlp_chunk(c, more):
                act.wait_ge(res_done, c + 1)
                if not (isinstance(c, int) and c == 0):
                    act.wait_ge(hid_done, HB * c)
                nc.scalar.activation(hid_t[:, :, :], res_ps[:, :, :], ACT.Copy, scale=1.0 / (NEIGH * H_SCALE))\
                    .then_inc(hid_in_ready, 1)
                if more:
                    copy_prep(c + 1)
                for b in range(HB):
                    act.wait_ge(hid_done, HB * c + b + 1)
                    if b == 0 and not (isinstance(c, int) and c == 0):
                        act.wait_ge(mlp_done, c)
                    nc.scalar.activation(act_t[:, b, :], hid_ps[:, b % 2, :], ACT.Relu, bias=b1_sb[:, b:b + 1])\
                        .then_inc(act_ready, 1)

            act.wait_ge(consts, 5)
            count_tile(0, 0)
            count_tile(0, 1)
            act.wait_ge(ln_ready, 1)
            nc.scalar.activation(ln1_set[3], ln1_set[2], ACT.Sqrt).then_inc(std1_done, 1)
            act.wait_ge(h_scaled, 1)
            for k in range(KT):
                nc.scalar.activation(x_all[:, k, :], x_all[:, k, :], ACT.Relu, bias=ln1_set[5][:, k, 1:2],
                                     scale=ln1_set[5][:, k, 0:1]).then_inc(h_relu, 1)
            count_tile(0, 2)
            count_tile(0, 3)
            act.wait_ge(w_loaded, 64)
            copy_prep(0)

            def chunk(c, first=False, more=True):
                if more:
                    for t in range(TC - 1):
                        count_tile(c + 1, t)
                if not first:
                    ln2_rows(c - 1)
                if more:
                    count_tile(c + 1, TC - 1)
                if not first:
                    copy_h2t(c - 1)
                mlp_chunk(c, more)

            chunk(0, first=True)
            with act.Fori(1, NC - 1) as c:
                chunk(c)
            chunk(NC - 1, more=False)
            ln2_rows(NC - 1)
            copy_h2t(NC - 1)

        @block.tensor
        def _(pe):
            def prep_chunk(c):
                pe.wait_ge(diag_ready, c + 1)
                if not (isinstance(c, int) and c == 0):
                    pe.wait_ge(thr_copied, c)
                for t in range(TC):
                    last = nc.tensor.matmul(thr_ps[:, t * P:(t + 1) * P], ones[:, :], thr_diag[:, t, :],
                                            start=True, stop=True)
                last.then_inc(thr_done, 1)
                if not (isinstance(c, int) and c == 0):
                    pe.wait_ge(fill_copied, c)
                if not (isinstance(c, int) and c < 2):
                    pe.wait_ge(h2_copied, DH * (c - 1))
                for t in range(TC):
                    last = nc.tensor.transpose(tr_ps[0:NEIGH, 0, t * P:(t + 1) * P], fill[:, t, :], ident16[:, :])
                last.then_inc(fill_tr_done, 1)

            def gather_tile(c, k):
                if isinstance(c, int) and c == 0 and k % 4 == 0:
                    pe.wait_ge(h_lo_done, k // 4 + 1)
                pe.wait_ge(st_ready, c * KT + k + 1)
                for h in range(DH):
                    for s in range(2):
                        last = nc.tensor.matmul(res_ps[:, h, :], h_j[:, k, s, h * P:(h + 1) * P],
                                                st[:, k % ST_RING, :], start=(k == 0 and s == 0), stop=False)
                last.then_inc(st_used, 1)

            def gather_rest(c):
                if isinstance(c, int) and c == 0:
                    pe.wait_ge(h16_loaded, 16)
                pe.wait_ge(fill_copied, c + 1)
                for h in range(DH):
                    for s in range(2):
                        nc.tensor.matmul(res_ps[:, h, :], h_16[:, s, h * P:(h + 1) * P], fill_t[:, :],
                                         start=False, stop=False)
                pe.wait_ge(hnat_loaded, 16 * (c + 1))
                for h in range(DH):
                    for t in range(TC):
                        for s in range(2):
                            last = nc.tensor.matmul(res_ps[:, h, t * P:(t + 1) * P], h_nat[:, t, s, h * P:(h + 1) * P],
                                                    sixteen_i[:, :], start=False,
                                                    stop=(t == TC - 1 and s == 1))
                last.then_inc(res_done, 1)

            def mlp_chunk(c):
                pe.wait_ge(hid_in_ready, c + 1)
                for b in range(HB):
                    if not (isinstance(c, int) and c == 0 and b < 2):
                        pe.wait_ge(act_ready, HB * c + b - 1)
                    for h in range(DH):
                        last = nc.tensor.matmul(hid_ps[:, b % 2, :], w1_sb[:, h, b * P:(b + 1) * P], hid_t[:, h, :],
                                                start=(h == 0), stop=(h == DH - 1))
                    last.then_inc(hid_done, 1)
                if not (isinstance(c, int) and c == 0):
                    pe.wait_ge(x2_added, c)
                pe.wait_ge(act_ready, HB * (c + 1))
                for t in range(TC):
                    nc.tensor.matmul(mlp_ps[:, t, :], ones[0:1, :], b2_sb[:, :], start=True, stop=False)
                    for b in range(HB):
                        last = nc.tensor.matmul(mlp_ps[:, t, :], act_t[:, b, t * P:(t + 1) * P], w2_sb[:, b, :],
                                                start=False, stop=(b == HB - 1))
                last.then_inc(mlp_done, 1)

            def transpose_h2(c):
                for h in range(DH):
                    for s, ready in enumerate((h2_hi, h2_lo)):
                        if h == 0:
                            pe.wait_ge(ready, c + 1)
                            if s == 0:
                                if not (isinstance(c, int) and c == 0):
                                    pe.wait_ge(h2_copied, DH * c)
                                pe.wait_ge(fill_copied, c + 2 if not last_chunk(c) else NC)
                        elif s == 0:
                            pe.wait_ge(h2_copied, DH * c + h)
                        for t in range(TC):
                            last = nc.tensor.transpose(tr_ps[:, s, t * P:(t + 1) * P],
                                                       h2_st[:, s, t, h * P:(h + 1) * P], ident16[:, :])
                    last.then_inc(h2_tr, 1)

            def last_chunk(c):
                return isinstance(c, int) and c == NC - 1

            def chunk(c, first=False, more=True):
                for k in range(KT):
                    gather_tile(c, k)
                    if not first and k == 21:
                        transpose_h2(c - 1)
                gather_rest(c)
                if more:
                    prep_chunk(c + 1)
                mlp_chunk(c)

            pe.wait_ge(consts, 5)
            prep_chunk(0)
            pe.wait_ge(w_loaded, 64)
            chunk(0, first=True)
            with pe.Fori(1, NC - 1) as c:
                chunk(c)
            chunk(NC - 1, more=False)
            transpose_h2(NC - 1)


def layer1(nc, adj, x2_dram, out, keep):
    with ExitStack() as ctx:
        def sb(name, shape, dt):
            return ctx.enter_context(nc.sbuf_tensor(name, shape, dt))

        def pb(name, shape, dt):
            return ctx.enter_context(nc.psum_tensor(name, shape, dt))

        def sem(name):
            return ctx.enter_context(nc.semaphore(name))

        ident, ones = keep["ident"], keep["ones"]
        h2t, v_hi, v_lo = keep["h2t"], keep["v_hi"], keep["v_lo"]
        a_sp, exp_scale, wvt = keep["a_sp"], keep["exp_scale"], keep["wvt"]
        KL = 4
        s_all = sb("s_all", [P, KT, CH], F32)
        adj_m = sb("adj_m", [P, 2, KL, CH], U8)
        not_adj = sb("not_adj", [P, 2, KL, CH], U8)
        t_q = sb("t_q", [P, DH, 2, CH], F16)
        t_next = sb("t_next", [P, DH, 2, CH], F16)
        t_32 = sb("t_32", [P, CH], F32)
        s_max = sb("s_max", [P, CH], F32)
        exp_bias = sb("exp_bias", [P, 1], F32)
        max_col = sb("max_col", [P, TC], F32)
        max_diag = sb("max_diag", [P, TC, P], F32)
        max_b = sb("max_b", [P, CH], F32)
        p_32 = sb("p_32", [P, X_RING, CH], F32)
        p_hi = sb("p_hi", [P, X_RING, CH], F16)
        p_lo = sb("p_lo", [P, X_RING, CH], F16)
        r_sum = sb("r_sum", [P, TC, 2], F32)
        o_n = sb("o_n", [P, TC, D], F32)
        o_t = sb("o_t", [P, DH, P], F32)
        x2_in = sb("x2_in", [P, TC, D], F32)
        o_out = sb("o_out", [P, TC, D], F32)
        pv_ps = [pb(f"pv_ps{t}", [P, CH], F32) for t in range(TC)]
        qk_ps = [pb(f"qk_ps{i}", [P, CH], F32) for i in range(QK_RING)]
        m_ps = [pb(f"m_ps{i}", [P, CH], F32) for i in range(2)]
        adj_loaded = [sem(f"adj_loaded{i}") for i in range(2)]
        bias_set = sem("bias_set")
        flipped, qk_done, masked, maxed = sem("flipped"), sem("qk_done"), sem("masked"), sem("maxed")
        t_done, t_rounded, t_split, t_copied, t_moved = sem("t_done"), sem("t_rounded"), sem("t_split"), sem("t_copied"), sem("t_moved")
        max_tr, max_red, max_dg, max_bc, max_ready = sem("max_tr"), sem("max_red"), sem("max_dg"), sem("max_bc"), sem("max_ready")
        shifted, exped, p_hi_done, p_lo_done, pv_done = sem("shifted"), sem("exped"), sem("p_hi_done"), sem("p_lo_done"), sem("pv_done")
        rs_chain, rs_ready, o_ready, o_tr, o_copied, proj_done = sem("rs_chain"), sem("rs_ready"), sem("o_ready"), sem("o_tr"), sem("o_copied"), sem("proj_done")
        out_ready, x2_loaded, out_stored = sem("out_ready"), sem("x2_loaded"), sem("out_stored")
        block = ctx.enter_context(nc.Block())

        LOADS = KT // KL
        T_AT = [1, 3]
        TR_AT = [4, 8, 12, 16]
        PROJ_AT = [6, 10, 14, 18]

        def is0(c, n=0):
            return isinstance(c, int) and c <= n

        @block.sync
        def _(sp):
            def load_adj(c, n, slot):
                if not (is0(c) and is0(n, 1)):
                    sp.wait_ge(flipped, c * LOADS + n - 1)
                sp.dma_start(adj_m[:, slot, :, :], adj[bass.ds(n * (KL * P), KL * P), bass.ds(c * CH, CH)]
                             .rearrange("(k p) q -> p k q", p=P)).then_inc(adj_loaded[slot], 16)

            def load_chunk(c):
                with sp.Fori(0, LOADS // 2) as m:
                    load_adj(c, m * 2, 0)
                    load_adj(c, m * 2 + 1, 1)

            def load_x2(c):
                if not is0(c):
                    sp.wait_ge(out_ready, TC * c)
                sp.dma_start(x2_in[:, :, :], x2_dram[bass.ds(c * CH, CH), :].rearrange("(t p) m -> p t m", p=P))\
                    .then_inc(x2_loaded, 16)

            def store(c):
                sp.wait_ge(out_ready, TC * (c + 1))
                sp.dma_start(out[bass.ds(c * CH, CH), :].rearrange("(t p) m -> p t m", p=P), o_out[:, :, :])\
                    .then_inc(out_stored, 16)

            for n in range(LOADS):
                load_adj(0, n, n % 2)
            load_x2(0)
            load_chunk(1)
            with sp.Fori(2, NC) as c:
                load_chunk(c)
                store(c - 2)
                load_x2(c - 1)
            store(NC - 2)
            load_x2(NC - 1)
            store(NC - 1)
            sp.wait_ge(out_stored, 16 * NC)

        @block.gpsimd
        def _(pool):
            nc.gpsimd.memset(exp_bias[:, :], math.log(P_SCALE)).then_inc(bias_set, 1)

            def low(c, k):
                slot = k % X_RING
                pool.wait_ge(p_hi_done, KT * c + k + 1)
                if not (is0(c) and k < X_RING):
                    pool.wait_ge(pv_done, KT * c + k - X_RING + 1)
                nc.gpsimd.tensor_tensor(p_lo[:, slot, :], p_32[:, slot, :], p_hi[:, slot, :], ALU.subtract)\
                    .then_inc(p_lo_done, 1)

            for k in range(KT):
                low(0, k)
            with pool.Fori(1, NC) as c:
                for k in range(KT):
                    low(c, k)

        @block.vector
        def _(dve):
            rs_seq = Chain(dve, rs_chain, 1)

            def split_t(c, h):
                dve.wait_ge(t_rounded, DH * c + h + 1)
                nc.vector.tensor_tensor(t_next[:, h, 1, :], t_32[:, :], t_next[:, h, 0, :], ALU.subtract)\
                    .then_inc(t_split, 1)

            def move_t(c):
                dve.wait_ge(t_split, DH * (c + 1))
                if not is0(c):
                    dve.wait_ge(qk_done, KT * c)
                nc.vector.tensor_copy(t_q[:, :, :, :], t_next[:, :, :, :]).then_inc(t_moved, 1)

            def flip(c, n):
                dve.wait_ge(adj_loaded[n % 2], 16 * (LOADS // 2 * c + n // 2 + 1))
                if not (is0(c) and n < 2):
                    dve.wait_ge(masked, KT * c + KL * (n - 1))
                nc.vector.tensor_single_scalar(
                    not_adj[:, n % 2, :, :].rearrange("p k q -> p (k q)").bitcast(U32),
                    adj_m[:, n % 2, :, :].rearrange("p k q -> p (k q)").bitcast(U32),
                    0x01010101, ALU.bitwise_xor).then_inc(flipped, 1)

            def mask(c, k):
                if k % KL == 0:
                    flip(c, k // KL)
                    dve.wait_ge(flipped, LOADS * c + k // KL + 1)
                if not is0(c):
                    dve.wait_ge(shifted, KT * (c - 1) + k + 1)
                dve.wait_ge(qk_done, KT * c + k + 1)
                nc.vector.scalar_tensor_tensor(s_all[:, k, :], not_adj[:, k // KL % 2, k % KL, :], NEG,
                                               qk_ps[k % QK_RING][:, :], ALU.mult, ALU.add).then_inc(masked, 1)

            def running_max(c, k):
                dve.wait_ge(masked, KT * c + k + 1)
                if not (is0(c) and k == 0):
                    dve.wait_ge(maxed, KT * c + k)
                if k == 0:
                    if not is0(c):
                        dve.wait_ge(max_tr, c)
                    nc.vector.tensor_copy(s_max[:, :], s_all[:, 0, :]).then_inc(maxed, 1)
                else:
                    nc.vector.tensor_tensor(s_max[:, :], s_max[:, :], s_all[:, k, :], ALU.max).then_inc(maxed, 1)

            def maxima(c):
                dve.wait_ge(max_tr, c + 1)
                nc.vector.tensor_reduce(out=max_col[:, :], in_=m_ps[0][:, :].rearrange("p (t k) -> p t k", t=TC),
                                        axis=AX.X, op=ALU.max).then_inc(max_red, 1)
                dve.wait_ge(max_red, 2 * c + 1)
                nc.vector.tensor_single_scalar(max_col[:, :], max_col[:, :], NEG_FLOOR, ALU.max).then_inc(max_red, 1)
                dve.wait_ge(max_red, 2 * c + 2)
                if not is0(c):
                    dve.wait_ge(max_bc, c)
                for t in range(TC):
                    nc.vector.tensor_scalar(max_diag[:, t, :], ident[:, :], max_col[:, t:t + 1], None, ALU.mult)\
                        .then_inc(max_dg, 1)

            def copy_max(c):
                dve.wait_ge(max_bc, c + 1)
                if not is0(c):
                    dve.wait_ge(shifted, KT * c)
                nc.vector.tensor_copy(max_b[:, :], m_ps[0][:, :]).then_inc(max_ready, 1)
                dve.wait_ge(max_ready, c + 1)

            def shift(c, k):
                if not (is0(c) and k < X_RING):
                    dve.wait_ge(p_lo_done, KT * c + k - X_RING + 1)
                    dve.wait_ge(p_hi_done, KT * c + k - X_RING + 1)
                nc.vector.tensor_tensor(p_32[:, k % X_RING, :], s_all[:, k, :], max_b[:, :], ALU.subtract)\
                    .then_inc(shifted, 1)

            def sums(c):
                dve.wait_ge(pv_done, KT * (c + 1))
                if not is0(c):
                    dve.wait_ge(o_ready, TC * c)
                rs_seq.begin(c)
                for t in range(TC):
                    last = nc.vector.tensor_single_scalar(r_sum[:, t, 0:1], pv_ps[t][:, D:D + 1], TINY, ALU.max)
                rs_seq.then(last)
                nc.vector.reciprocal(r_sum[:, :, 1], r_sum[:, :, 0]).then_inc(rs_ready, 1)
                rs_seq.end()

            def add_x2(c, t):
                dve.wait_ge(proj_done, TC * c + t + 1)
                if t == 0:
                    dve.wait_ge(x2_loaded, 16 * (c + 1))
                    if not is0(c):
                        dve.wait_ge(out_stored, 16 * c)
                nc.vector.tensor_tensor(o_out[:, t, :], m_ps[1][:, D:2 * D], x2_in[:, t, :], ALU.add)\
                    .then_inc(out_ready, 1)

            def chunk(c, first=False, more=True, more2=True):
                shift(c, 0)
                for k in range(KT):
                    if more:
                        mask(c + 1, k)
                    if k + 1 < KT:
                        shift(c, k + 1)
                    if more:
                        running_max(c + 1, k)
                    if not first and k == 0:
                        sums(c - 1)
                    if more2 and k - 2 in T_AT:
                        split_t(c + 2, T_AT.index(k - 2))
                    if not first and k - 1 in PROJ_AT:
                        add_x2(c - 1, PROJ_AT.index(k - 1))
                if more2:
                    move_t(c + 2)
                if more:
                    maxima(c + 1)
                    copy_max(c + 1)

            for h in range(DH):
                split_t(0, h)
            move_t(0)
            for k in range(KT):
                mask(0, k)
                if k >= 1:
                    running_max(0, k - 1)
                if k - 2 in T_AT:
                    split_t(1, T_AT.index(k - 2))
            running_max(0, KT - 1)
            move_t(1)
            maxima(0)
            copy_max(0)
            chunk(0, first=True)
            with dve.Fori(1, NC - 2) as c:
                chunk(c)
            chunk(NC - 2, more2=False)
            chunk(NC - 1, more=False, more2=False)
            sums(NC - 1)
            for t in range(TC):
                add_x2(NC - 1, t)

        @block.scalar
        def _(act):
            def round_t(c, h):
                act.wait_ge(t_done, DH * c + h + 1)
                if not (is0(c) and h == 0):
                    act.wait_ge(t_split, DH * c + h)
                nc.scalar.activation(t_32[:, :], m_ps[0][:, :], ACT.Copy, scale=1.0 / H_SCALE)\
                    .then_inc(t_copied, 1)
                act.wait_ge(t_copied, DH * c + h + 1)
                if not is0(c) and h == 0:
                    act.wait_ge(t_moved, c)
                nc.scalar.activation(t_next[:, h, 0, :], t_32[:, :], ACT.Copy).then_inc(t_rounded, 1)

            def exps(c, k):
                act.wait_ge(shifted, KT * c + k + 1)
                slot = k % X_RING
                nc.scalar.activation(p_32[:, slot, :], p_32[:, slot, :], ACT.Exp, bias=exp_bias[:, :],
                                     scale=exp_scale[:, :])\
                    .then_inc(exped, 1)
                act.wait_ge(exped, KT * c + k + 1)
                if not (is0(c) and k < X_RING):
                    act.wait_ge(pv_done, KT * c + k - X_RING + 1)
                nc.scalar.activation(p_hi[:, slot, :], p_32[:, slot, :], ACT.Copy)\
                    .then_inc(p_hi_done, 1)

            def evacuate(c):
                act.wait_ge(rs_ready, c + 1)
                if not is0(c):
                    act.wait_ge(o_tr, TC * c)
                for t in range(TC):
                    nc.scalar.activation(o_n[:, t, :], pv_ps[t][:, 0:D], ACT.Copy, scale=r_sum[:, t, 1:2])\
                        .then_inc(o_ready, 1)

            def copy_ot(c, t):
                act.wait_ge(o_tr, TC * c + t + 1)
                if not (is0(c) and t == 0):
                    act.wait_ge(proj_done, TC * c + t)
                nc.scalar.activation(o_t[:, :, :], m_ps[1][:, 0:D].rearrange("p (h q) -> p h q", h=DH), ACT.Copy)\
                    .then_inc(o_copied, 1)

            def chunk(c, first=False, more2=True):
                for k in range(KT):
                    exps(c, k)
                    if not first and k == 0:
                        evacuate(c - 1)
                    if more2 and k - 1 in T_AT:
                        round_t(c + 2, T_AT.index(k - 1))
                    if not first and k - 1 in TR_AT:
                        copy_ot(c - 1, TR_AT.index(k - 1))

            act.wait_ge(bias_set, 1)
            for c in range(2):
                for h in range(DH):
                    round_t(c, h)
            chunk(0, first=True)
            with act.Fori(1, NC - 2) as c:
                chunk(c)
            chunk(NC - 2, more2=False)
            chunk(NC - 1, more2=False)
            evacuate(NC - 1)
            for t in range(TC):
                copy_ot(NC - 1, t)

        @block.tensor
        def _(pe):
            def t_product(c, h):
                if not (is0(c) and h == 0):
                    pe.wait_ge(t_copied, DH * c + h)
                if not is0(c, 1):
                    pe.wait_ge(max_ready, c - 1)
                n = 0
                for o in range(DH):
                    for s, u in ((0, 0), (0, 1), (1, 0)):
                        last = nc.tensor.matmul(m_ps[0][:, :], a_sp[:, o, s, h * P:(h + 1) * P],
                                                h2t[:, o, u, bass.ds(c * CH, CH)], start=(n == 0), stop=(n == 5))
                        n += 1
                last.then_inc(t_done, 1)

            def scores(c, k):
                if k == 0:
                    pe.wait_ge(t_moved, c + 1)
                if not (is0(c) and k < QK_RING):
                    pe.wait_ge(masked, KT * c + k - QK_RING + 1)
                n = 0
                for h in range(DH):
                    for s, u in ((0, 0), (0, 1), (1, 0)):
                        last = nc.tensor.matmul(qk_ps[k % QK_RING][:, :], h2t[:, h, s, k * P:(k + 1) * P],
                                                t_q[:, h, u, :], start=(n == 0), stop=(n == 5))
                        n += 1
                last.then_inc(qk_done, 1)

            def values(c, k):
                pe.wait_ge(p_lo_done, KT * c + k + 1)
                if k == 0 and not is0(c):
                    pe.wait_ge(o_ready, TC * c)
                slot = k % X_RING
                for t in range(TC):
                    q = slice(t * P, (t + 1) * P)
                    nc.tensor.matmul(pv_ps[t][:, 0:D + 1], p_hi[:, slot, q], v_hi[:, k, 0:D + 1],
                                     start=(k == 0), stop=False)
                    nc.tensor.matmul(pv_ps[t][:, 0:D], p_hi[:, slot, q], v_lo[:, k, :], start=False, stop=False,
                                     skip_group_check=True)
                    last = nc.tensor.matmul(pv_ps[t][:, 0:D + 1], p_lo[:, slot, q], v_hi[:, k, 0:D + 1],
                                            start=False, stop=(k == KT - 1))
                last.then_inc(pv_done, 1)

            def transpose_max(c):
                pe.wait_ge(maxed, KT * (c + 1))
                if not (isinstance(c, int) and c == NC - 1):
                    pe.wait_ge(t_copied, DH * (c + 2))
                for t in range(TC):
                    last = nc.tensor.transpose(m_ps[0][:, t * P:(t + 1) * P], s_max[:, t * P:(t + 1) * P], ident[:, :])
                last.then_inc(max_tr, 1)

            def spread_max(c):
                pe.wait_ge(max_dg, TC * (c + 1))
                for t in range(TC):
                    last = nc.tensor.matmul(m_ps[0][:, t * P:(t + 1) * P], ones[:, :], max_diag[:, t, :],
                                            start=True, stop=True)
                last.then_inc(max_bc, 1)

            def transpose_o(c, t):
                pe.wait_ge(o_ready, TC * (c + 1))
                if not (is0(c) and t == 0):
                    pe.wait_ge(out_ready, TC * c + t)
                for h in range(DH):
                    last = nc.tensor.transpose(m_ps[1][:, h * P:(h + 1) * P], o_n[:, t, h * P:(h + 1) * P], ident[:, :])
                last.then_inc(o_tr, 1)

            def project(c, t):
                pe.wait_ge(o_copied, TC * c + t + 1)
                for h in range(DH):
                    last = nc.tensor.matmul(m_ps[1][:, D:2 * D], o_t[:, h, :], wvt[:, h, :],
                                            start=(h == 0), stop=(h == DH - 1))
                last.then_inc(proj_done, 1)

            def chunk(c, first=False, more=True, more2=True):
                for k in range(KT):
                    if more:
                        scores(c + 1, k)
                    if more2 and k in T_AT:
                        t_product(c + 2, T_AT.index(k))
                    if k >= LAG:
                        values(c, k - LAG)
                    if not first and k in TR_AT:
                        transpose_o(c - 1, TR_AT.index(k))
                    if not first and k in PROJ_AT:
                        project(c - 1, PROJ_AT.index(k))
                for k in range(KT - LAG, KT):
                    if more and k == KT - LAG + 1:
                        transpose_max(c + 1)
                    if more and k == KT - LAG + 3:
                        spread_max(c + 1)
                    values(c, k)

            for h in range(DH):
                t_product(0, h)
            for k in range(KT):
                scores(0, k)
                if k in T_AT:
                    t_product(1, T_AT.index(k))
            transpose_max(0)
            spread_max(0)
            chunk(0, first=True)
            with pe.Fori(1, NC - 2) as c:
                chunk(c)
            chunk(NC - 2, more2=False)
            chunk(NC - 1, more=False, more2=False)
            for t in range(TC):
                transpose_o(NC - 1, t)
                project(NC - 1, t)


_INS = ["x", "adj", "L0_gnn_W1", "L0_gnn_b1", "L0_gnn_W2", "L0_gnn_b2", "L1_gnn_Wq", "L1_gnn_Wk", "L1_gnn_Wv"]


def kernel(**inputs):
    import numpy as _np
    import concourse.bacc as _bacc
    from concourse import mybir as _mybir
    from concourse.bass_utils import run_bass_kernel_spmd as _run

    nc = _bacc.Bacc("TRN2", target_bir_lowering=False, num_devices=1)
    arrays, args = {}, []
    for name in _INS:
        a = _np.ascontiguousarray(inputs[name])
        if a.dtype == _np.bool_:
            a = a.view(_np.uint32)
        arrays[f"in_{name}"] = a
        args.append(nc.dram_tensor(f"in_{name}", a.shape, _mybir.dt.from_np(a.dtype), kind="ExternalInput").ap())
    out = nc.dram_tensor("out_x", (4096, 256), _mybir.dt.float32, kind="ExternalOutput").ap()
    args[1] = args[1].bitcast(_mybir.dt.uint8)
    build(nc, *args, out)
    r = _run(nc, [arrays], core_ids=[0])
    return r.results[0]["out_x"]
```

```python
import math
from contextlib import ExitStack
import concourse.bass as bass
from concourse import mybir

F32, F16, U8 = mybir.dt.float32, mybir.dt.float16, mybir.dt.uint8
I32, U32 = mybir.dt.int32, mybir.dt.uint32
ALU, ACT, AX = mybir.AluOpType, mybir.ActivationFunctionType, mybir.AxisListType

P = 128
N, D, HID = 4096, 256, 512
CH = 512
NC = N // CH
KT = N // P
TC = CH // P
DH = D // P
HB = HID // P
GR = 4
GW = N // GR
NW = GW // 128
NEIGH = 16
PAIRS = N // 2
EPS = 1e-5
SCAN_AT = [2, 5, 7, 16]
H_SCALE = 2048.0
P_SCALE = 16384.0
NEG = -1.0e30
NEG_FLOOR = -5.0e29
TINY = 1e-30
ST_RING, X_RING, QK_RING = 8, 8, 2
LAG = 5
V_W = D + 2


class Chain:

    def __init__(self, engine, sem, per):
        self.engine, self.sem, self.per = engine, sem, per

    def begin(self, chunk):
        self.chunk, self.n = chunk, 0

    def then(self, instruction):
        instruction.then_inc(self.sem, 1)
        self.n += 1
        self.engine.wait_ge(self.sem, self.chunk * self.per + self.n)

    def end(self):
        assert self.n == self.per, (self.n, self.per)


def build(nc, x, adj, w1, b1, w2, b2, wq, wk, wv, out):
    x2_dram = nc.dram_tensor("x2_scratch", (N, D), F32, kind="Internal").ap()
    h_dram = nc.dram_tensor("h_scratch", (N, 2 * D), F16, kind="Internal").ap()
    with ExitStack() as ctx:
        mem = Memory(nc, ctx)
        sync0, pool0, vector0, scalar0, tensor0 = layer0(nc, mem, x, adj, w1, b1, w2, b2, wq, wk, wv, h_dram, x2_dram)
        sync1, pool1, vector1, scalar1, tensor1 = layer1(nc, mem, adj, x2_dram, out)
        block = ctx.enter_context(nc.Block())

        @block.sync
        def _(sp):
            sync1(sp, sync0(sp))

        @block.gpsimd
        def _(pool):
            pool0(pool)
            pool1(pool)

        @block.vector
        def _(dve):
            vector1(dve, vector0(dve))

        @block.scalar
        def _(act):
            scalar1(act, scalar0(act))

        @block.tensor
        def _(pe):
            tensor1(pe, tensor0(pe))


class Memory:

    BIG, SMALL = 64 * 1024, 52 * 1024

    def __init__(self, nc, ctx):
        self.nc, self.ctx = nc, ctx
        self.h2t = self.sb("h2t", [P, DH, 2, N], F16)
        self.v_hi = self.sb("v_hi", [P, KT, V_W], F16)
        self.v_lo = self.sb("v_lo", [P, KT, D], F16)
        self.ident = self.sb("ident", [P, P], F32)
        self.ones = self.sb("ones", [P, P], F32)
        self.ident16 = self.sb("ident16", [P, P], F16)
        self.a_sp = self.sb("a_sp", [P, DH, 2, D], F16)
        self.exp_scale = self.sb("exp_scale", [P, 1], F32)
        self.wvt = self.sb("wvt", [P, DH, D], F32)
        self.big = self.sb("big", [P, self.BIG], U8)
        self.small = self.sb("small", [P, self.SMALL], U8)
        self.adj_pair = self.sb("adj_pair", [P, 2, N], U8)
        self.rows_a = self.sb("rows_a", [P, TC, D], F32)
        self.rows_b = self.sb("rows_b", [P, TC, D], F32)
        self.rows_c = self.sb("rows_c", [P, TC, D], F32)
        self.banks = ctx.enter_context(nc.psum_tensor("banks", [P, 8, CH], F32))

    def sb(self, name, shape, dt):
        return self.ctx.enter_context(self.nc.sbuf_tensor(name, shape, dt))

    def sem(self, name):
        return self.ctx.enter_context(self.nc.semaphore(name))


class Cut:

    def __init__(self, place):
        self.place, self.at = place, 0

    def __call__(self, shape, dt):
        size = {F32: 4, F16: 2, U8: 1, mybir.dt.int8: 1}[dt] * math.prod(shape)
        part = self.place[:, self.at:self.at + size].bitcast(dt)
        self.at += size
        names = "abcd"[:len(shape)]
        return part.rearrange(f"p ({' '.join(names)}) -> p {' '.join(names)}",
                              **dict(zip(names[1:], shape[1:]))) if len(shape) > 1 else part


def layer0(nc, mem, x, adj, w1, b1, w2, b2, wq, wk, wv, h_dram, x2_dram):
    sb, sem = mem.sb, mem.sem
    ident, ones, ident16 = mem.ident, mem.ones, mem.ident16
    h2t, v_hi, v_lo = mem.h2t, mem.v_hi, mem.v_lo
    a_sp, exp_scale, wvt = mem.a_sp, mem.exp_scale, mem.wvt
    cut = Cut(mem.big)
    h_j = cut([KT, 2, D], F16)
    adj_t = cut([NW, CH, 4], U8)
    adj_blk = cut([CH // 32, GW], U8)
    assert cut.at == mem.BIG
    cut = Cut(mem.small)
    st = cut([ST_RING, CH], F16)
    act_t = cut([HB, CH], F32)
    w1_sb = cut([DH, HID], F32)
    w2_sb = cut([HB, D], F32)
    cum = cut([2, PAIRS], F16)
    hid_t = cut([DH, CH], F32)
    h_nat = cut([TC, 2, D], F16)
    sign_out = cut([PAIRS], mybir.dt.int8)
    thr_diag = cut([TC, P], F32)
    thr_b = cut([CH], F32)
    h_16 = cut([2, D], F16)[0:NEIGH, :, :]
    fill_t = cut([CH], F16)[0:NEIGH, :]
    h2_st = cut([2, TC, D], F16)
    assert cut.at <= mem.SMALL
    adj_nat = mem.adj_pair
    x_in, x2_sb, h32 = mem.rows_a, mem.rows_b, mem.rows_c
    b1_sb = sb("b1_sb", [P, HB], F32)
    b2_b = sb("b2_b", [P, D], F32)
    sixteen_i = sb("sixteen_i", [P, P], F16)
    j_col = sb("j_col", [P, KT], F32)
    j_int = sb("j_int", [P, KT], I32)
    half_col = sb("half_col", [P, 2], F32)
    acc = sb("acc", [P, TC, 2], F32)
    thr = sb("thr", [P, 3, TC], F32)
    fill_na = sb("fill_na", [P, NEIGH], F32)
    fill_rank = sb("fill_rank", [P, NEIGH], F32)
    fill_zero = sb("fill_zero", [P, NEIGH], F32)
    fill_need = sb("fill_need", [P, 1], F32)
    fill = sb("fill", [P, TC, NEIGH], F16)
    stats = sb("stats", [P, TC, 6], F32)
    mv = sb("mv", [P, TC, 2], F32)
    rs = sb("rs", [P, TC, 2], F32)
    var = sb("var", [P, TC], F32)
    wait_pad = sb("wait_pad", [P, 1], F32)
    std = sb("std", [P, TC], F32)
    inv = sb("inv", [P, TC, 2], F32)
    x_all = h2t[:, :, :, :].rearrange("p h s n -> p (h s n)").bitcast(F32).rearrange("p (k m) -> p k m", k=KT)
    scratch = v_lo[:, :, :].rearrange("p k m -> p (k m)").bitcast(F32)

    def part(at, width):
        return scratch[:, at * KT:(at + width) * KT].rearrange("p (t n) -> p t n", n=width)
    ln1_set = (part(0, 6), part(6, 2), part(8, 1)[:, :, 0], part(9, 1)[:, :, 0], part(10, 2), part(12, 2))
    ln2_set = (stats, mv, var[:, :], std[:, :], inv, rs)
    wq_sb, wk_sb, wv_sb, a_f = (act_t[:, i, :].rearrange("p (h d) -> p h d", h=DH) for i in range(4))
    b2_sb = st.rearrange("p s n -> p (s n)").bitcast(F32)[0:1, 0:D]
    a_abs = sb("a_abs", [P, 4], F32)
    sc = sb("sc", [1, 4], F32)
    res_ps = mem.banks[:, 0:2, :]
    hid_ps = mem.banks[:, 2:4, :]
    mlp_ps = mem.banks[:, 4:6, :].rearrange("p b (t d) -> p (b t) d", d=D)
    thr_ps = mem.banks[:, 6, :]
    tr_ps = mem.banks[:, 7, :].bitcast(F16).rearrange("p (s n) -> p s n", s=2)
    a_ps = mem.banks[:, 2, :].rearrange("p (h d) -> p h d", h=DH)
    wvt_ps = mem.banks[:, 3, :].rearrange("p (h d) -> p h d", h=DH)
    m_ps = mem.banks[:, 4, 0:P + 1]
    b2_ps = mem.banks[:, 5, 0:D]
    w_loaded = sem("mlp_weights_loaded")
    x_loaded = [sem(f"x_loaded{i}") for i in range(2)]
    qkv_loaded, shared_consts, zeroed = sem("qkv_loaded"), sem("shared_consts"), sem("zeroed")
    a_done, wvt_done, b2_done, row_done, bc_done = sem("a_done"), sem("wvt_done"), sem("b2_done"), sem("row_done"), sem("bc_done")
    max_ready, scale_ready, setup_chain, setup_done, b2_ready = sem("a_max_ready"), sem("scale_ready"), sem("setup_chain"), sem("setup_done"), sem("b2_ready")
    xin_biased = sem("xin_biased")
    consts = sem("l0_consts")
    pool_chain = sem("l0_pool_chain")
    h_scaled, h_hi_done, h_lo_done, h_stored = sem("h_scaled"), sem("h_hi_done"), sem("h_lo_done"), sem("h_stored")
    h_relu, h16_loaded, ln_ready = sem("h_relu"), sem("h16_loaded"), sem("ln_ready")
    ln1_chain, prep_chain, ln2_chain = sem("ln1_chain"), sem("prep_chain"), sem("ln2_chain")
    nat_loaded = [sem(f"nat_loaded{i}") for i in range(2)]
    blk_loaded, scanned, transposed, counted = sem("blk_loaded"), sem("scanned"), sem("transposed"), sem("counted")
    tile_read, diag_ready, fill_ready = sem("tile_read"), sem("diag_ready"), sem("fill_ready")
    thr_done, fill_tr_done, thr_copied, fill_copied = sem("thr_done"), sem("fill_tr_done"), sem("thr_copied"), sem("fill_copied")
    st_ready, st_used, hnat_loaded, res_done = sem("st_ready"), sem("st_used"), sem("hnat_loaded"), sem("res_done")
    hid_in_ready, hid_done, act_ready, mlp_done = sem("hid_in_ready"), sem("hid_done"), sem("act_ready"), sem("mlp_done")
    xin_loaded, x2_added, x2_stored = sem("xin_loaded"), sem("x2_added"), sem("x2_stored")
    std1_done, std2_done, var2_ready = sem("std1_done"), sem("std2_done"), sem("var2_ready")
    ln2_ready, h2_relu, h2_hi, h2_lo = sem("ln2_ready"), sem("h2_relu"), sem("h2_hi"), sem("h2_lo")
    h2_tr, h2_copied, v_stored = sem("h2_tr"), sem("h2_copied"), sem("v_stored")

    def rows(t, c):
        return t[bass.ds(c * CH, CH), :].rearrange("(t p) m -> p t m", p=P)

    def sync(sp):
        def load_nat(c, t):
            n = c * TC + t
            if not (isinstance(c, int) and n < 2):
                sp.wait_ge(scanned, n - 1)
                sp.wait_ge(tile_read, n - 1)
            sp.dma_start(adj_nat[:, t % 2, :], adj[bass.ds(c * CH + t * P, P), :]).then_inc(nat_loaded[t % 2], 16)

        def load_blk(c):
            if not (isinstance(c, int) and c == 0):
                sp.wait_ge(transposed, c)
            for g in range(GR):
                src = adj[bass.ds(c * CH, CH), g * GW:(g + 1) * GW].rearrange("(i c) m -> c i m", c=32)
                sp.dma_start(adj_blk[32 * g:32 * (g + 1), :, :], src).then_inc(blk_loaded, 16)

        load_nat(0, 0)
        load_nat(0, 1)
        for dst, src in ((wq_sb, wq), (wk_sb, wk), (wv_sb, wv)):
            sp.dma_start(dst, src.rearrange("(o p) d -> p o d", p=P)).then_inc(qkv_loaded, 16)
        HW = NW // 2

        def in_k_order(t, half, g, m):
            return t[g * GW + half * HW * P:g * GW + (half + 1) * HW * P, :]\
                .rearrange("(w r b) m -> r w (b m)", r=32, b=4)

        for half in range(2):
            for g in range(GR):
                sp.dma_start(x_all[32 * g:32 * (g + 1), 16 * half:16 * (half + 1), :]
                             .rearrange("p (w b) m -> p w (b m)", b=4), in_k_order(x, half, g, D))\
                    .then_inc(x_loaded[half], 16)
            load_nat(0, 2 + half)
        load_blk(0)
        sp.dma_start(b1_sb[:, :], b1.rearrange("(o p) -> p o", p=P), allow_slow_non_contiguous=True).then_inc(w_loaded, 16)
        sp.dma_start(b2_sb, b2.rearrange("(a n) -> a n", a=1)).then_inc(w_loaded, 16)
        sp.dma_start(w1_sb, w1.rearrange("(o p) n -> p o n", p=P)).then_inc(w_loaded, 16)
        sp.dma_start(w2_sb, w2.rearrange("(o p) n -> p o n", p=P)).then_inc(w_loaded, 16)
        for half in range(2):
            sp.wait_ge(h_hi_done, HW * (half + 1))
            sp.wait_ge(h_lo_done, HW * (half + 1))
            for g in range(GR):
                sp.dma_start(in_k_order(h_dram, half, g, 2 * D), h_j[32 * g:32 * (g + 1), 16 * half:16 * (half + 1), :, :]
                             .rearrange("p (w b) s m -> p w (b s m)", b=4)).then_inc(h_stored, 16)
        sp.wait_ge(h_stored, 16 * GR * 2)
        sp.dma_start(h_16, h_dram[0:NEIGH, :].rearrange("p (s m) -> p s m", s=2)).then_inc(h16_loaded, 16)
        load_nat(1, 0)
        load_nat(1, 1)
        load_blk(1)

        def chunk(c, first=False, more=True, more2=True):
            if not first:
                sp.wait_ge(res_done, c)
            sp.dma_start(h_nat[:, :, :, :], h_dram[bass.ds(c * CH, CH), :]
                         .rearrange("(t p) (s m) -> p t s m", p=P, s=2)).then_inc(hnat_loaded, 16)
            if more:
                load_nat(c + 1, 2)
                load_nat(c + 1, 3)
            if more2:
                load_nat(c + 2, 0)
            if not first:
                finish_rows(c - 1)
            sp.dma_start(x_in[:, :, :], rows(x, c)).then_inc(xin_loaded, 16)
            if not first:
                store_values(c - 1)
            if more2:
                load_nat(c + 2, 1)
                load_blk(c + 2)

        def finish_rows(c):
            sp.wait_ge(x2_added, c + 1)
            sp.dma_start(rows(x2_dram, c), x2_sb[:, :, :]).then_inc(x2_stored, 16)

        def store_values(c):
            sp.wait_ge(h2_hi, c + 1)
            sp.wait_ge(h2_lo, c + 1)
            sp.dma_start(v_hi[:, bass.ds(c * TC, TC), 0:D], h2_st[:, 0, :, :]).then_inc(v_stored, 16)
            sp.dma_start(v_lo[:, bass.ds(c * TC, TC), :], h2_st[:, 1, :, :]).then_inc(v_stored, 16)

        chunk(0, first=True)
        with sp.Fori(1, NC - 2) as c:
            chunk(c)
        chunk(NC - 2, more2=False)
        chunk(NC - 1, more=False, more2=False)


        def adjacency_read():
            sp.wait_ge(scanned, TC * NC)
            sp.wait_ge(tile_read, TC * NC)

        def values_stored():
            store_values(NC - 1)
            sp.wait_ge(x2_stored, 16 * NC)
            sp.wait_ge(v_stored, 32 * NC)

        return adjacency_read, (lambda: finish_rows(NC - 1)), values_stored

    def pool(pool):
        nc.gpsimd.memset(ident[:, :], 0.0).then_inc(zeroed, 1)
        nc.gpsimd.memset(ident16[:, :], 0.0).then_inc(zeroed, 1)
        nc.gpsimd.memset(ones[:, :], 1.0).then_inc(shared_consts, 1)
        nc.gpsimd.memset(v_hi[:, :, D:V_W], 1.0).then_inc(shared_consts, 1)
        pool.wait_ge(zeroed, 2)
        for m in (ident, ident16):
            nc.gpsimd.affine_select(out=m[:, :], in_=m[:, :], compare_op=ALU.not_equal, fill=1.0,
                                    base=0, pattern=[[-1, P]], channel_multiplier=1).then_inc(shared_consts, 1)
        nc.gpsimd.iota(j_int[:, :], pattern=[[P, NW], [1, 4]], base=0, channel_multiplier=4).then_inc(consts, 1)
        nc.gpsimd.memset(half_col[:, 0:1], NEIGH - 0.5).then_inc(consts, 1)
        nc.gpsimd.memset(half_col[:, 1:2], NEIGH + 0.5).then_inc(consts, 1)
        nc.gpsimd.memset(fill_zero[:, :], 0.0).then_inc(consts, 1)
        nc.gpsimd.memset(sixteen_i[:, :], 0.0).then_inc(pool_chain, 1)
        pool.wait_ge(pool_chain, 1)
        nc.gpsimd.affine_select(out=sixteen_i[:, :], in_=sixteen_i[:, :], compare_op=ALU.not_equal,
                                fill=float(NEIGH), base=0, pattern=[[-1, P]], channel_multiplier=1)\
            .then_inc(consts, 1)
        for w in range(NW):
            k = slice(4 * w, 4 * (w + 1))
            pool.wait_ge(h_hi_done, w + 1)
            nc.gpsimd.tensor_tensor(h_j[:, k, 1, :], x_all[:, k, :], h_j[:, k, 0, :], ALU.subtract)\
                .then_inc(h_lo_done, 1)

        def ln2_low(c):
            pool.wait_ge(h2_hi, c + 1)
            if not (isinstance(c, int) and c == 0):
                pool.wait_ge(v_stored, 32 * c)
                pool.wait_ge(h2_tr, 2 * c)
            nc.gpsimd.tensor_tensor(h2_st[:, 1, :, :], h32[:, :, :], h2_st[:, 0, :, :], ALU.subtract)\
                .then_inc(h2_lo, 1)

        def bias_rows(c):
            pool.wait_ge(xin_loaded, 16 * (c + 1))
            for t in range(TC):
                nc.gpsimd.tensor_tensor(x_in[:, t, :], x_in[:, t, :], b2_b[:, :], ALU.add).then_inc(xin_biased, 1)

        pool.wait_ge(b2_ready, 1)
        bias_rows(0)
        bias_rows(1)
        ln2_low(0)
        with pool.Fori(2, NC) as c:
            bias_rows(c)
            ln2_low(c - 1)
        ln2_low(NC - 1)

    def vector(dve):
        ln1 = Chain(dve, ln1_chain, 6)
        prep = Chain(dve, prep_chain, 4 * TC + 4)
        ln2 = Chain(dve, ln2_chain, 6)

        def row_var(src, chain, ready, at, tiles, arrived=None):
            stats, mv, var = at[0:3]
            for t in range(tiles):
                if arrived and t % 16 == 0:
                    dve.wait_ge(arrived[t // 16], 16 * GR)
                last = nc.vector.bn_stats(stats[:, t, :], src[:, t, :])
            chain.then(last)
            nc.vector.memset(wait_pad[:, :], 0.0)
            for t in range(tiles):
                last = nc.vector.bn_aggr(mv[:, t, :], stats[:, t, :])
            chain.then(last)
            nc.vector.tensor_single_scalar(var, mv[:, :, 1], EPS, ALU.add).then_inc(ready, 1)

        def row_scale(chain, done, before, at):
            mv, var, std, inv, rs = at[1:]
            dve.wait_ge(done, before)
            chain.then(nc.vector.reciprocal(inv[:, :, 0], std))
            chain.then(nc.vector.tensor_tensor(inv[:, :, 1], inv[:, :, 0], inv[:, :, 0], ALU.mult))
            chain.then(nc.vector.scalar_tensor_tensor(inv[:, :, 1], inv[:, :, 1], -0.5 * H_SCALE, var,
                                                      ALU.mult, ALU.mult))
            chain.then(nc.vector.scalar_tensor_tensor(rs[:, :, 0], inv[:, :, 1], 1.5 * H_SCALE, inv[:, :, 0],
                                                      ALU.add, ALU.mult))
            return nc.vector.scalar_tensor_tensor(rs[:, :, 1], mv[:, :, 0], -1.0, rs[:, :, 0],
                                                  ALU.mult, ALU.mult)

        def scan_tile(c, t):
            n = c * TC + t
            dve.wait_ge(nat_loaded[t % 2], 16 * (c * 2 + t // 2 + 1))
            if not (isinstance(c, int) and n < 2):
                dve.wait_ge(counted, 2 * (n - 1))
            if t == 0 and not (isinstance(c, int) and c == 0):
                dve.wait_ge(fill_tr_done, c)
            pairs = adj_nat[:, t % 2, :].rearrange("p (n b) -> p n b", b=2)
            nc.vector.tensor_tensor_scan(cum[:, t % 2, :], pairs[:, :, 0], pairs[:, :, 1], 0.0,
                                         ALU.add, ALU.add).then_inc(scanned, 1)
            nc.vector.tensor_scalar(fill_na[:, :], adj_nat[:, t % 2, 0:NEIGH], -1.0, 1.0, ALU.mult, ALU.add)\
                .then_inc(tile_read, 1)
            dve.wait_ge(tile_read, n + 1)
            prep.then(nc.vector.tensor_tensor_scan(fill_rank[:, :], fill_na[:, :], fill_zero[:, :], 0.0,
                                                   ALU.add, ALU.add))
            dve.wait_ge(scanned, n + 1)
            prep.then(nc.vector.tensor_scalar(fill_need[:, :], cum[:, t % 2, PAIRS - 1:PAIRS], -1.0,
                                              float(NEIGH), ALU.mult, ALU.add))
            prep.then(nc.vector.scalar_tensor_tensor(fill[:, t, :], fill_rank[:, :], fill_need[:, :],
                                                     fill_na[:, :], ALU.is_le, ALU.mult))

        def transpose_chunk(c):
            dve.wait_ge(blk_loaded, 16 * GR * (c + 1))
            if not (isinstance(c, int) and c == 0):
                dve.wait_ge(st_ready, KT * c)
            src = adj_blk[:, :, :].bitcast(U32)
            dst = adj_t[:, :, :, :].rearrange("p w i b -> p (w i b)").bitcast(U32)\
                .rearrange("p (w i) -> p w i", w=NW)
            for i in range(CH // 32):
                last = nc.vector.transpose(dst[:, :, 32 * i:32 * (i + 1)],
                                           src[:, i, :].rearrange("p (w r) -> p w r", w=NW))
            last.then_inc(transposed, 1)
            dve.wait_ge(transposed, c + 1)

        def thresholds(c):
            dve.wait_ge(counted, 2 * TC * (c + 1))
            prep.then(nc.vector.tensor_scalar(thr[:, 0:2, :].rearrange("p s t -> p t s"), acc[:, :, :],
                                              float(PAIRS), 0.5, ALU.add, ALU.mult))
            prep.then(nc.vector.tensor_tensor(thr[:, 1, :], thr[:, 1, :], thr[:, 0, :], ALU.subtract))
            prep.then(nc.vector.tensor_single_scalar(thr[:, 1, :], thr[:, 1, :], 1.0, ALU.min))
            prep.then(nc.vector.scalar_tensor_tensor(thr[:, 2, :], thr[:, 0, :], 2.0, thr[:, 1, :],
                                                     ALU.mult, ALU.add))
            for t in range(TC):
                prep.then(nc.vector.tensor_scalar(thr_diag[:, t, :], ident[:, :], thr[:, 2, t:t + 1], None,
                                                  ALU.mult))
            prep.end()

        def select_tile(c, k):
            if not (isinstance(c, int) and c == 0 and k < ST_RING):
                dve.wait_ge(st_used, c * KT + k - ST_RING + 1)
            nc.vector.scalar_tensor_tensor(st[:, k % ST_RING, :], thr_b[:, :], j_col[:, k:k + 1],
                                           adj_t[:, k // 4, :, k % 4], ALU.is_ge, ALU.mult)\
                .then_inc(st_ready, 1)

        def ln2_stats(c):
            ln2.begin(c)
            dve.wait_ge(mlp_done, c + 1)
            dve.wait_ge(xin_biased, TC * (c + 1))
            if not (isinstance(c, int) and c == 0):
                dve.wait_ge(x2_stored, 16 * c)
            nc.vector.tensor_tensor(x2_sb[:, :, :], mlp_ps[:, :, :], x_in[:, :, :], ALU.add).then_inc(x2_added, 1)
            dve.wait_ge(x2_added, c + 1)
            if not (isinstance(c, int) and c == 0):
                dve.wait_ge(h2_relu, TC * c)
            row_var(x2_sb, ln2, var2_ready, ln2_set, TC)

        def ln2_scale(c):
            row_scale(ln2, std2_done, c + 1, ln2_set).then_inc(ln2_ready, 1)
            ln2.end()

        dve.wait_ge(consts, 5)
        for g in range(GR):
            last = nc.vector.tensor_single_scalar(j_col[32 * g:32 * (g + 1), :], j_int[32 * g:32 * (g + 1), :],
                                                  float((GW - P) * g), ALU.add)
        last.then_inc(consts, 1)
        def chunk(c, first=False, more=True):
            if more:
                prep.begin(c + 1)
            dve.wait_ge(thr_copied, c + 1)
            for k in range(KT):
                select_tile(c, k)
                if more and k in SCAN_AT:
                    scan_tile(c + 1, SCAN_AT.index(k))
                if not first and k == 9:
                    ln2_stats(c - 1)
                if not first and k == 12:
                    ln2_scale(c - 1)
            if more:
                thresholds_and_signal(c + 1)
                transpose_chunk(c + 1)

        def thresholds_and_signal(c):
            thresholds(c)
            nc.vector.sem_inc(diag_ready, 1)

        setup = Chain(dve, setup_chain, 9)
        setup.begin(0)

        def setup_max():
            dve.wait_ge(a_done, 1)
            setup.then(nc.vector.tensor_copy(a_f, a_ps))
            nc.vector.tensor_reduce(out=a_abs[:, 0:1], in_=a_f, axis=AX.XY, op=ALU.max,
                                    apply_absolute_value=True).then_inc(max_ready, 1)
            dve.wait_ge(wvt_done, 1)
            nc.vector.tensor_single_scalar(wvt[:, :, :], wvt_ps, 1.0 / H_SCALE, ALU.mult).then_inc(setup_done, 1)

        def setup_scale():
            dve.wait_ge(row_done, 1)
            setup.then(nc.vector.tensor_reduce(out=sc[0:1, 0:1], in_=m_ps[0:1, 0:P], axis=AX.X, op=ALU.max))
            setup.then(nc.vector.tensor_scalar(sc[0:1, 0:1], sc[0:1, 0:1], 2.0 ** -40, 1.0 / 128, ALU.max, ALU.mult))
            setup.then(nc.vector.reciprocal(sc[0:1, 1:2], sc[0:1, 0:1]))
            nc.vector.tensor_single_scalar(sc[0:1, 2:3].bitcast(U32), sc[0:1, 1:2].bitcast(U32), 0x7F800000,
                                           ALU.bitwise_and).then_inc(scale_ready, 1)

        def setup_split():
            dve.wait_ge(bc_done, 1)
            setup.then(nc.vector.tensor_copy(a_abs[:, 2:3], m_ps[:, P:P + 1]))
            setup.then(nc.vector.tensor_single_scalar(a_abs[:, 3:4], a_abs[:, 2:3], H_SCALE, ALU.mult))
            setup.then(nc.vector.reciprocal(exp_scale[:, :], a_abs[:, 3:4]))
            setup.then(nc.vector.tensor_scalar(a_f, a_f, a_abs[:, 2:3], None, ALU.mult))
            setup.then(nc.vector.tensor_copy(a_sp[:, :, 0, :], a_f))
            nc.vector.tensor_tensor(a_sp[:, :, 1, :], a_f, a_sp[:, :, 0, :], ALU.subtract).then_inc(setup_done, 1)
            setup.end()

        prep.begin(0)
        dve.wait_ge(shared_consts, 4)
        scan_tile(0, 0)
        scan_tile(0, 1)
        setup_max()
        scan_tile(0, 2)
        setup_scale()
        scan_tile(0, 3)
        setup_split()
        ln1.begin(0)
        row_var(x_all, ln1, ln_ready, ln1_set, KT, x_loaded)
        row_scale(ln1, std1_done, 1, ln1_set).then_inc(h_scaled, 1)
        ln1.end()
        thresholds_and_signal(0)
        transpose_chunk(0)
        for w in range(NW):
            dve.wait_ge(h_relu, 4 * (w + 1))
            nc.vector.tensor_copy(h_j[:, 4 * w:4 * (w + 1), 0, :], x_all[:, 4 * w:4 * (w + 1), :])\
                .then_inc(h_hi_done, 1)
        chunk(0, first=True)
        with dve.Fori(1, NC - 1) as c:
            chunk(c)
        chunk(NC - 1, more=False)
        return (lambda: ln2_stats(NC - 1)), (lambda: ln2_scale(NC - 1))

    def scalar(act):
        def relu_rows(src, done):
            for t in range(TC):
                nc.scalar.activation(h32[:, t, :], src[:, t, :], ACT.Relu, bias=rs[:, t, 1:2],
                                     scale=rs[:, t, 0:1]).then_inc(done, 1)

        def count_tile(c, t):
            act.wait_ge(scanned, c * TC + t + 1)
            if t == 0 and not (isinstance(c, int) and c == 0):
                act.wait_ge(diag_ready, c)
            for s in range(2):
                n = 2 * (c * TC + t) + s
                if not (isinstance(c, int) and n == 0):
                    act.wait_ge(counted, n)
                nc.scalar.activation(sign_out[:, :], cum[:, t % 2, :], ACT.Sign, bias=half_col[:, s:s + 1],
                                     scale=-1.0, accum_out=acc[:, t, s:s + 1]).then_inc(counted, 1)

        def copy_prep(c):
            act.wait_ge(thr_done, c + 1)
            nc.scalar.activation(thr_b[:, :], thr_ps[:, :], ACT.Copy).then_inc(thr_copied, 1)
            act.wait_ge(fill_tr_done, c + 1)
            nc.scalar.activation(fill_t[:, :], tr_ps[0:NEIGH, 0, :], ACT.Copy).then_inc(fill_copied, 1)

        def ln2_std(c):
            act.wait_ge(var2_ready, c + 1)
            nc.scalar.activation(std[:, :], var[:, :], ACT.Sqrt).then_inc(std2_done, 1)

        def ln2_rows(c):
            act.wait_ge(ln2_ready, c + 1)
            if not (isinstance(c, int) and c == 0):
                act.wait_ge(h2_lo, c)
            relu_rows(x2_sb, h2_relu)
            act.wait_ge(h2_relu, TC * (c + 1))
            if not (isinstance(c, int) and c == 0):
                act.wait_ge(v_stored, 32 * c)
                act.wait_ge(h2_tr, 2 * c)
            nc.scalar.activation(h2_st[:, 0, :, :], h32[:, :, :], ACT.Copy).then_inc(h2_hi, 1)

        def copy_h2t(c):
            for h in range(DH):
                act.wait_ge(h2_tr, DH * c + h + 1)
                nc.scalar.activation(h2t[:, h, :, bass.ds(c * CH, CH)], tr_ps[:, :, :], ACT.Copy)\
                    .then_inc(h2_copied, 1)

        def mlp_in(c):
            act.wait_ge(res_done, c + 1)
            if not (isinstance(c, int) and c == 0):
                act.wait_ge(hid_done, HB * c)
            nc.scalar.activation(hid_t[:, :, :], res_ps[:, :, :], ACT.Copy, scale=1.0 / (NEIGH * H_SCALE))\
                .then_inc(hid_in_ready, 1)

        def mlp_relu(c):
            for b in range(HB):
                act.wait_ge(hid_done, HB * c + b + 1)
                if b == 0 and not (isinstance(c, int) and c == 0):
                    act.wait_ge(mlp_done, c)
                nc.scalar.activation(act_t[:, b, :], hid_ps[:, b % 2, :], ACT.Relu, bias=b1_sb[:, b:b + 1])\
                    .then_inc(act_ready, 1)

        act.wait_ge(consts, 5)
        for t in range(TC):
            count_tile(0, t)
        act.wait_ge(b2_done, 1)
        nc.scalar.activation(b2_b[:, :], b2_ps, ACT.Copy).then_inc(b2_ready, 1)
        act.wait_ge(ln_ready, 1)
        nc.scalar.activation(ln1_set[3], ln1_set[2], ACT.Sqrt).then_inc(std1_done, 1)
        act.wait_ge(h_scaled, 1)
        for k in range(KT):
            nc.scalar.activation(x_all[:, k, :], x_all[:, k, :], ACT.Relu, bias=ln1_set[5][:, k, 1:2],
                                 scale=ln1_set[5][:, k, 0:1]).then_inc(h_relu, 1)
            if k == 7:
                copy_prep(0)
        act.wait_ge(w_loaded, 64)

        def chunk(c, first=False, more=True):
            if more:
                for t in range(TC - 1):
                    count_tile(c + 1, t)
            if not first:
                ln2_std(c - 1)
                ln2_rows(c - 1)
            if more:
                count_tile(c + 1, TC - 1)
            if not first:
                copy_h2t(c - 1)
            mlp_in(c)
            if more:
                copy_prep(c + 1)
                mlp_relu(c)

        chunk(0, first=True)
        with act.Fori(1, NC - 1) as c:
            chunk(c)
        chunk(NC - 1, more=False)
        return [lambda step=step: step(NC - 1) for step in (mlp_relu, ln2_std, ln2_rows, copy_h2t)]

    def tensor(pe):
        def prep_chunk(c):
            pe.wait_ge(diag_ready, c + 1)
            if not (isinstance(c, int) and c == 0):
                pe.wait_ge(thr_copied, c)
            for t in range(TC):
                last = nc.tensor.matmul(thr_ps[:, t * P:(t + 1) * P], ones[:, :], thr_diag[:, t, :],
                                        start=True, stop=True)
            last.then_inc(thr_done, 1)
            if not (isinstance(c, int) and c == 0):
                pe.wait_ge(fill_copied, c)
            if not (isinstance(c, int) and c < 2):
                pe.wait_ge(h2_copied, DH * (c - 1))
            for t in range(TC):
                last = nc.tensor.transpose(tr_ps[0:NEIGH, 0, t * P:(t + 1) * P], fill[:, t, :], ident16[:, :])
            last.then_inc(fill_tr_done, 1)

        def gather_tile(c, k):
            if isinstance(c, int) and c == 0 and k % 4 == 0:
                pe.wait_ge(h_lo_done, k // 4 + 1)
            pe.wait_ge(st_ready, c * KT + k + 1)
            for h in range(DH):
                for s in range(2):
                    last = nc.tensor.matmul(res_ps[:, h, :], h_j[:, k, s, h * P:(h + 1) * P],
                                            st[:, k % ST_RING, :], start=(k == 0 and s == 0), stop=False)
            last.then_inc(st_used, 1)

        def gather_rest(c):
            if isinstance(c, int) and c == 0:
                pe.wait_ge(h16_loaded, 16)
            pe.wait_ge(fill_copied, c + 1)
            for h in range(DH):
                for s in range(2):
                    nc.tensor.matmul(res_ps[:, h, :], h_16[:, s, h * P:(h + 1) * P], fill_t[:, :],
                                     start=False, stop=False)
            pe.wait_ge(hnat_loaded, 16 * (c + 1))
            for h in range(DH):
                for t in range(TC):
                    for s in range(2):
                        last = nc.tensor.matmul(res_ps[:, h, t * P:(t + 1) * P], h_nat[:, t, s, h * P:(h + 1) * P],
                                                sixteen_i[:, :], start=False,
                                                stop=(t == TC - 1 and s == 1))
            last.then_inc(res_done, 1)

        def mlp_up(c):
            if isinstance(c, int) and c == 0:
                pe.wait_ge(setup_done, 2)
            pe.wait_ge(hid_in_ready, c + 1)
            for b in range(HB):
                if not (isinstance(c, int) and c == 0 and b < 2):
                    pe.wait_ge(act_ready, HB * c + b - 1)
                for h in range(DH):
                    last = nc.tensor.matmul(hid_ps[:, b % 2, :], w1_sb[:, h, b * P:(b + 1) * P], hid_t[:, h, :],
                                            start=(h == 0), stop=(h == DH - 1))
                last.then_inc(hid_done, 1)

        def mlp_down(c):
            if not (isinstance(c, int) and c == 0):
                pe.wait_ge(x2_added, c)
            pe.wait_ge(act_ready, HB * (c + 1))
            for t in range(TC):
                for b in range(HB):
                    last = nc.tensor.matmul(mlp_ps[:, t, :], act_t[:, b, t * P:(t + 1) * P], w2_sb[:, b, :],
                                            start=(b == 0), stop=(b == HB - 1))
            last.then_inc(mlp_done, 1)

        def transpose_h2(c):
            for h in range(DH):
                for s, ready in enumerate((h2_hi, h2_lo)):
                    if h == 0:
                        pe.wait_ge(ready, c + 1)
                        if s == 0:
                            if not (isinstance(c, int) and c == 0):
                                pe.wait_ge(h2_copied, DH * c)
                            pe.wait_ge(fill_copied, c + 2 if not last_chunk(c) else NC)
                    elif s == 0:
                        pe.wait_ge(h2_copied, DH * c + h)
                    for t in range(TC):
                        last = nc.tensor.transpose(tr_ps[:, s, t * P:(t + 1) * P],
                                                   h2_st[:, s, t, h * P:(h + 1) * P], ident16[:, :])
                last.then_inc(h2_tr, 1)

        def last_chunk(c):
            return isinstance(c, int) and c == NC - 1

        def chunk(c, first=False, more=True):
            for k in range(KT):
                gather_tile(c, k)
                if not first and k == 21:
                    transpose_h2(c - 1)
            gather_rest(c)
            if more:
                prep_chunk(c + 1)
            mlp_up(c)
            mlp_down(c)

        pe.wait_ge(qkv_loaded, 48)
        for h in range(DH):
            for o in range(DH):
                last = nc.tensor.matmul(a_ps[:, h, :], wq_sb[:, o, h * P:(h + 1) * P], wk_sb[:, o, :],
                                        start=(o == 0), stop=(o == DH - 1))
        last.then_inc(a_done, 1)
        pe.wait_ge(shared_consts, 4)
        for h in range(DH):
            for o in range(DH):
                last = nc.tensor.transpose(wvt_ps[:, h, o * P:(o + 1) * P], wv_sb[:, o, h * P:(h + 1) * P], ident[:, :])
        last.then_inc(wvt_done, 1)
        pe.wait_ge(max_ready, 1)
        nc.tensor.transpose(m_ps[0:1, 0:P], a_abs[:, 0:1], ident[:, :]).then_inc(row_done, 1)
        pe.wait_ge(scale_ready, 1)
        nc.tensor.matmul(m_ps[:, P:P + 1], ones[0:1, :], sc[0:1, 2:3], start=True, stop=True).then_inc(bc_done, 1)
        pe.wait_ge(w_loaded, 64)
        nc.tensor.matmul(b2_ps, ones[0:1, :], b2_sb, start=True, stop=True).then_inc(b2_done, 1)
        pe.wait_ge(consts, 5)
        prep_chunk(0)
        chunk(0, first=True)
        with pe.Fori(1, NC - 1) as c:
            chunk(c)
        pe.wait_ge(setup_done, 2)
        for k in range(KT):
            gather_tile(NC - 1, k)
            if k == 21:
                transpose_h2(NC - 2)
        gather_rest(NC - 1)

        def h2_there():
            pe.wait_ge(h2_copied, DH * NC)
            pe.wait_ge(v_stored, 32 * NC)

        return (lambda: mlp_up(NC - 1)), (lambda: mlp_down(NC - 1)), (lambda: transpose_h2(NC - 1)), h2_there

    return sync, pool, vector, scalar, tensor


def layer1(nc, mem, adj, x2_dram, out):
    sb, sem = mem.sb, mem.sem
    ident, ones = mem.ident, mem.ones
    h2t, v_hi, v_lo = mem.h2t, mem.v_hi, mem.v_lo
    a_sp, exp_scale, wvt = mem.a_sp, mem.exp_scale, mem.wvt
    KL = 4
    s_all = Cut(mem.big)([KT, CH], F32)
    cut = Cut(mem.small)
    t_q = cut([DH, 2, CH], F16)
    t_next = cut([DH, 2, CH], F16)
    p_32 = cut([X_RING, CH], F32)
    p_hi = cut([X_RING, CH], F16)
    p_lo = cut([X_RING, CH], F16)
    s_max = cut([CH], F32)
    max_diag = cut([TC, P], F32)
    t_32 = cut([CH], F32)
    max_b = cut([CH], F32)
    o_t = cut([TC, DH, P], F32)[:, :, :, :]
    assert cut.at <= mem.SMALL
    cut = Cut(mem.adj_pair[:, :, :].rearrange("p s n -> p (s n)"))
    adj_m = cut([2, KL, CH], U8)
    not_adj = cut([2, KL, CH], U8)
    x2_in, o_out, o_n = mem.rows_a, mem.rows_b, mem.rows_c
    exp_bias = sb("exp_bias", [P, 1], F32)
    max_col = sb("max_col", [P, TC], F32)
    r_sum = sb("r_sum", [P, TC, 2], F32)
    pv_ps = [mem.banks[:, i, :] for i in (0, 1, 4, 5)]
    qk_ps = [mem.banks[:, i, :] for i in (2, 3)]
    m_ps = [mem.banks[:, i, :] for i in (6, 7)]
    TAIL_PS = [m_ps[1], m_ps[0]] + qk_ps
    adj_loaded = [sem(f"adj_loaded{i}") for i in range(2)]
    bias_set = sem("bias_set")
    flipped, qk_done, masked, maxed = sem("flipped"), sem("qk_done"), sem("masked"), sem("maxed")
    t_done, t_rounded, t_split, t_copied, t_moved = sem("t_done"), sem("t_rounded"), sem("t_split"), sem("t_copied"), sem("t_moved")
    max_tr, max_red, max_dg, max_bc, max_ready = sem("max_tr"), sem("max_red"), sem("max_dg"), sem("max_bc"), sem("max_ready")
    shifted, exped, p_hi_done, p_lo_done, pv_done = sem("shifted"), sem("exped"), sem("p_hi_done"), sem("p_lo_done"), sem("pv_done")
    rs_chain, rs_ready, o_ready, o_tr, o_copied, proj_done = sem("rs_chain"), sem("rs_ready"), sem("o_ready"), sem("o_tr"), sem("o_copied"), sem("proj_done")
    out_ready, x2_loaded, out_stored = sem("out_ready"), sem("x2_loaded"), sem("out_stored")

    LOADS = KT // KL
    T_AT = [1, 3]
    TR_AT = [4, 8, 12, 16]
    PROJ_AT = [6, 10, 14, 18]

    def is0(c, n=0):
        return isinstance(c, int) and c <= n

    def sync(sp, finish):
        def load_adj(c, n, slot):
            if not (is0(c) and is0(n, 1)):
                sp.wait_ge(flipped, c * LOADS + n - 1)
            sp.dma_start(adj_m[:, slot, :, :], adj[bass.ds(n * (KL * P), KL * P), bass.ds(c * CH, CH)]
                         .rearrange("(k p) q -> p k q", p=P)).then_inc(adj_loaded[slot], 16)

        def load_chunk(c):
            with sp.Fori(0, LOADS // 2) as m:
                load_adj(c, m * 2, 0)
                load_adj(c, m * 2 + 1, 1)

        def load_x2(c):
            if not is0(c):
                sp.wait_ge(out_ready, TC * c)
            sp.dma_start(x2_in[:, :, :], x2_dram[bass.ds(c * CH, CH), :].rearrange("(t p) m -> p t m", p=P))\
                .then_inc(x2_loaded, 16)

        def store(c):
            sp.wait_ge(out_ready, TC * (c + 1))
            sp.dma_start(out[bass.ds(c * CH, CH), :].rearrange("(t p) m -> p t m", p=P), o_out[:, :, :])\
                .then_inc(out_stored, 16)

        adjacency_read, finish_rows, values_stored = finish
        adjacency_read()
        for n in range(LOADS):
            load_adj(0, n, n % 2)
            if n == 1:
                finish_rows()
            if n == 3:
                values_stored()
        load_x2(0)
        load_chunk(1)
        with sp.Fori(2, NC) as c:
            load_chunk(c)
            store(c - 2)
            load_x2(c - 1)
        store(NC - 2)
        load_x2(NC - 1)
        for t in range(TC):
            sp.wait_ge(out_ready, TC * (NC - 1) + t + 1)
            sp.dma_start(out[(NC - 1) * CH + t * P:(NC - 1) * CH + (t + 1) * P, :], o_out[:, t, :])\
                .then_inc(out_stored, 16)
        sp.wait_ge(out_stored, 16 * (NC - 1) + 16 * TC)

    def pool(pool):
        nc.gpsimd.memset(exp_bias[:, :], math.log(P_SCALE)).then_inc(bias_set, 1)

        def low(c, k):
            slot = k % X_RING
            pool.wait_ge(p_hi_done, KT * c + k + 1)
            if not (is0(c) and k < X_RING):
                pool.wait_ge(pv_done, KT * c + k - X_RING + 1)
            nc.gpsimd.tensor_tensor(p_lo[:, slot, :], p_32[:, slot, :], p_hi[:, slot, :], ALU.subtract)\
                .then_inc(p_lo_done, 1)

        for k in range(KT):
            low(0, k)
        with pool.Fori(1, NC) as c:
            for k in range(KT):
                low(c, k)

    def vector(dve, finish):
        rs_seq = Chain(dve, rs_chain, 1)

        def split_t(c, h):
            dve.wait_ge(t_rounded, DH * c + h + 1)
            nc.vector.tensor_tensor(t_next[:, h, 1, :], t_32[:, :], t_next[:, h, 0, :], ALU.subtract)\
                .then_inc(t_split, 1)

        def move_t(c):
            dve.wait_ge(t_split, DH * (c + 1))
            if not is0(c):
                dve.wait_ge(qk_done, KT * c)
            nc.vector.tensor_copy(t_q[:, :, :, :], t_next[:, :, :, :]).then_inc(t_moved, 1)

        def flip(c, n):
            dve.wait_ge(adj_loaded[n % 2], 16 * (LOADS // 2 * c + n // 2 + 1))
            if not (is0(c) and n < 2):
                dve.wait_ge(masked, KT * c + KL * (n - 1))
            nc.vector.tensor_single_scalar(
                not_adj[:, n % 2, :, :].rearrange("p k q -> p (k q)").bitcast(U32),
                adj_m[:, n % 2, :, :].rearrange("p k q -> p (k q)").bitcast(U32),
                0x01010101, ALU.bitwise_xor).then_inc(flipped, 1)

        def mask(c, k):
            if k % KL == 0:
                flip(c, k // KL)
                dve.wait_ge(flipped, LOADS * c + k // KL + 1)
            if not is0(c):
                dve.wait_ge(shifted, KT * (c - 1) + k + 1)
            dve.wait_ge(qk_done, KT * c + k + 1)
            nc.vector.scalar_tensor_tensor(s_all[:, k, :], not_adj[:, k // KL % 2, k % KL, :], NEG,
                                           qk_ps[k % QK_RING][:, :], ALU.mult, ALU.add).then_inc(masked, 1)

        def running_max(c, k):
            dve.wait_ge(masked, KT * c + k + 1)
            if not (is0(c) and k == 0):
                dve.wait_ge(maxed, KT * c + k)
            if k == 0:
                if not is0(c):
                    dve.wait_ge(max_tr, c)
                nc.vector.tensor_copy(s_max[:, :], s_all[:, 0, :]).then_inc(maxed, 1)
            else:
                nc.vector.tensor_tensor(s_max[:, :], s_max[:, :], s_all[:, k, :], ALU.max).then_inc(maxed, 1)

        def maxima(c):
            dve.wait_ge(max_tr, c + 1)
            nc.vector.tensor_reduce(out=max_col[:, :], in_=m_ps[0][:, :].rearrange("p (t k) -> p t k", t=TC),
                                    axis=AX.X, op=ALU.max).then_inc(max_red, 1)
            dve.wait_ge(max_red, 2 * c + 1)
            nc.vector.tensor_single_scalar(max_col[:, :], max_col[:, :], NEG_FLOOR, ALU.max).then_inc(max_red, 1)
            dve.wait_ge(max_red, 2 * c + 2)
            if not is0(c):
                dve.wait_ge(max_bc, c)
            for t in range(TC):
                nc.vector.tensor_scalar(max_diag[:, t, :], ident[:, :], max_col[:, t:t + 1], None, ALU.mult)\
                    .then_inc(max_dg, 1)

        def copy_max(c):
            dve.wait_ge(max_bc, c + 1)
            if not is0(c):
                dve.wait_ge(shifted, KT * c)
            nc.vector.tensor_copy(max_b[:, :], m_ps[0][:, :]).then_inc(max_ready, 1)
            dve.wait_ge(max_ready, c + 1)

        def shift(c, k):
            if not (is0(c) and k < X_RING):
                dve.wait_ge(p_lo_done, KT * c + k - X_RING + 1)
                dve.wait_ge(p_hi_done, KT * c + k - X_RING + 1)
            nc.vector.tensor_tensor(p_32[:, k % X_RING, :], s_all[:, k, :], max_b[:, :], ALU.subtract)\
                .then_inc(shifted, 1)

        def sums(c):
            dve.wait_ge(pv_done, KT * (c + 1))
            if not is0(c):
                dve.wait_ge(o_ready, TC * c)
            rs_seq.begin(c)
            for t in range(TC):
                last = nc.vector.tensor_single_scalar(r_sum[:, t, 0:1], pv_ps[t][:, D:D + 1], TINY, ALU.max)
            rs_seq.then(last)
            nc.vector.reciprocal(r_sum[:, :, 1], r_sum[:, :, 0]).then_inc(rs_ready, 1)
            rs_seq.end()

        def add_x2(c, t, bank=m_ps[1]):
            dve.wait_ge(proj_done, TC * c + t + 1)
            if t == 0:
                dve.wait_ge(x2_loaded, 16 * (c + 1))
                if not is0(c):
                    dve.wait_ge(out_stored, 16 * c)
            nc.vector.tensor_tensor(o_out[:, t, :], bank[:, D:2 * D], x2_in[:, t, :], ALU.add)\
                .then_inc(out_ready, 1)

        def chunk(c, first=False, more=True, more2=True):
            shift(c, 0)
            for k in range(KT):
                if more:
                    mask(c + 1, k)
                if k + 1 < KT:
                    shift(c, k + 1)
                if more:
                    running_max(c + 1, k)
                if not first and k == 0:
                    sums(c - 1)
                if more2 and k - 2 in T_AT:
                    split_t(c + 2, T_AT.index(k - 2))
                if not first and k - 1 in PROJ_AT:
                    add_x2(c - 1, PROJ_AT.index(k - 1))
            if more2:
                move_t(c + 2)
            if more:
                maxima(c + 1)
                copy_max(c + 1)

        ln2_stats, ln2_scale = finish
        for h in range(DH):
            split_t(0, h)
        move_t(0)
        ln2_stats()
        for k in range(KT):
            mask(0, k)
            if k == 2:
                ln2_scale()
            if k >= 1:
                running_max(0, k - 1)
            if k - 2 in T_AT:
                split_t(1, T_AT.index(k - 2))
        running_max(0, KT - 1)
        move_t(1)
        maxima(0)
        copy_max(0)
        chunk(0, first=True)
        with dve.Fori(1, NC - 2) as c:
            chunk(c)
        chunk(NC - 2, more2=False)
        chunk(NC - 1, more=False, more2=False)
        sums(NC - 1)
        for t in range(TC):
            add_x2(NC - 1, t, TAIL_PS[t])

    def scalar(act, finish):
        def round_t(c, h):
            act.wait_ge(t_done, DH * c + h + 1)
            if not (is0(c) and h == 0):
                act.wait_ge(t_split, DH * c + h)
            nc.scalar.activation(t_32[:, :], m_ps[0][:, :], ACT.Copy, scale=1.0 / H_SCALE)\
                .then_inc(t_copied, 1)
            act.wait_ge(t_copied, DH * c + h + 1)
            if not is0(c) and h == 0:
                act.wait_ge(t_moved, c)
            nc.scalar.activation(t_next[:, h, 0, :], t_32[:, :], ACT.Copy).then_inc(t_rounded, 1)

        def exps(c, k):
            act.wait_ge(shifted, KT * c + k + 1)
            slot = k % X_RING
            nc.scalar.activation(p_32[:, slot, :], p_32[:, slot, :], ACT.Exp, bias=exp_bias[:, :],
                                 scale=exp_scale[:, :])\
                .then_inc(exped, 1)
            act.wait_ge(exped, KT * c + k + 1)
            if not (is0(c) and k < X_RING):
                act.wait_ge(pv_done, KT * c + k - X_RING + 1)
            nc.scalar.activation(p_hi[:, slot, :], p_32[:, slot, :], ACT.Copy)\
                .then_inc(p_hi_done, 1)

        def evacuate(c):
            act.wait_ge(rs_ready, c + 1)
            if not is0(c):
                act.wait_ge(o_tr, TC * c)
            for t in range(TC):
                nc.scalar.activation(o_n[:, t, :], pv_ps[t][:, 0:D], ACT.Copy, scale=r_sum[:, t, 1:2])\
                    .then_inc(o_ready, 1)

        def copy_ot(c, t, bank=m_ps[1]):
            act.wait_ge(o_tr, TC * c + t + 1)
            if bank is m_ps[1] and not (is0(c) and t == 0):
                act.wait_ge(proj_done, TC * c + t)
            nc.scalar.activation(o_t[:, t, :, :], bank[:, 0:D].rearrange("p (h q) -> p h q", h=DH), ACT.Copy)\
                .then_inc(o_copied, 1)

        def chunk(c, first=False, more2=True):
            for k in range(KT):
                exps(c, k)
                if not first and k == 0:
                    evacuate(c - 1)
                if more2 and k - 1 in T_AT:
                    round_t(c + 2, T_AT.index(k - 1))
                if not first and k - 1 in TR_AT:
                    copy_ot(c - 1, TR_AT.index(k - 1))

        mlp_relu, ln2_std, ln2_rows, copy_h2t = finish
        round_t(0, 0)
        mlp_relu()
        round_t(0, 1)
        round_t(1, 0)
        ln2_std()
        round_t(1, 1)
        ln2_rows()
        copy_h2t()
        act.wait_ge(bias_set, 1)
        chunk(0, first=True)
        with act.Fori(1, NC - 2) as c:
            chunk(c)
        chunk(NC - 2, more2=False)
        chunk(NC - 1, more2=False)
        evacuate(NC - 1)
        for t in range(TC):
            copy_ot(NC - 1, t, TAIL_PS[t])

    def tensor(pe, finish):
        def t_product(c, h):
            if not (is0(c) and h == 0):
                pe.wait_ge(t_copied, DH * c + h)
            if not is0(c, 1):
                pe.wait_ge(max_ready, c - 1)
            n = 0
            for o in range(DH):
                for s, u in ((0, 0), (0, 1), (1, 0)):
                    last = nc.tensor.matmul(m_ps[0][:, :], a_sp[:, o, s, h * P:(h + 1) * P],
                                            h2t[:, o, u, bass.ds(c * CH, CH)], start=(n == 0), stop=(n == 5))
                    n += 1
            last.then_inc(t_done, 1)

        def scores(c, k):
            if k == 0:
                pe.wait_ge(t_moved, c + 1)
            if not (is0(c) and k < QK_RING):
                pe.wait_ge(masked, KT * c + k - QK_RING + 1)
            n = 0
            for h in range(DH):
                for s, u in ((0, 0), (0, 1), (1, 0)):
                    last = nc.tensor.matmul(qk_ps[k % QK_RING][:, :], h2t[:, h, s, k * P:(k + 1) * P],
                                            t_q[:, h, u, :], start=(n == 0), stop=(n == 5))
                    n += 1
            last.then_inc(qk_done, 1)

        def values(c, k):
            pe.wait_ge(p_lo_done, KT * c + k + 1)
            if k == 0 and not is0(c):
                pe.wait_ge(o_ready, TC * c)
            slot = k % X_RING
            for t in range(TC):
                q = slice(t * P, (t + 1) * P)
                nc.tensor.matmul(pv_ps[t][:, 0:D + 1], p_hi[:, slot, q], v_hi[:, k, 0:D + 1],
                                 start=(k == 0), stop=False)
                nc.tensor.matmul(pv_ps[t][:, 0:D], p_hi[:, slot, q], v_lo[:, k, :], start=False, stop=False,
                                 skip_group_check=True)
                last = nc.tensor.matmul(pv_ps[t][:, 0:D + 1], p_lo[:, slot, q], v_hi[:, k, 0:D + 1],
                                        start=False, stop=(k == KT - 1))
            last.then_inc(pv_done, 1)

        def transpose_max(c):
            pe.wait_ge(maxed, KT * (c + 1))
            if not (isinstance(c, int) and c == NC - 1):
                pe.wait_ge(t_copied, DH * (c + 2))
            for t in range(TC):
                last = nc.tensor.transpose(m_ps[0][:, t * P:(t + 1) * P], s_max[:, t * P:(t + 1) * P], ident[:, :])
            last.then_inc(max_tr, 1)

        def spread_max(c):
            pe.wait_ge(max_dg, TC * (c + 1))
            for t in range(TC):
                last = nc.tensor.matmul(m_ps[0][:, t * P:(t + 1) * P], ones[:, :], max_diag[:, t, :],
                                        start=True, stop=True)
            last.then_inc(max_bc, 1)

        def transpose_o(c, t, bank=m_ps[1]):
            pe.wait_ge(o_ready, TC * (c + 1))
            if bank is m_ps[1] and not (is0(c) and t == 0):
                pe.wait_ge(out_ready, TC * c + t)
            for h in range(DH):
                last = nc.tensor.transpose(bank[:, h * P:(h + 1) * P], o_n[:, t, h * P:(h + 1) * P], ident[:, :])
            last.then_inc(o_tr, 1)

        def project(c, t, bank=m_ps[1]):
            pe.wait_ge(o_copied, TC * c + t + 1)
            for h in range(DH):
                last = nc.tensor.matmul(bank[:, D:2 * D], o_t[:, t, h, :], wvt[:, h, :],
                                        start=(h == 0), stop=(h == DH - 1))
            last.then_inc(proj_done, 1)

        def chunk(c, first=False, more=True, more2=True):
            for k in range(KT):
                if more:
                    scores(c + 1, k)
                if more2 and k in T_AT:
                    t_product(c + 2, T_AT.index(k))
                if k >= LAG:
                    values(c, k - LAG)
                if not first and k in TR_AT:
                    transpose_o(c - 1, TR_AT.index(k))
                if not first and k in PROJ_AT:
                    project(c - 1, PROJ_AT.index(k))
            for k in range(KT - LAG, KT):
                if more and k == KT - LAG + 1:
                    transpose_max(c + 1)
                if more and k == KT - LAG + 3:
                    spread_max(c + 1)
                values(c, k)

        mlp_up, mlp_down, transpose_h2, h2_there = finish
        t_product(0, 0)
        mlp_up()
        t_product(0, 1)
        mlp_down()
        for k in range(KT):
            if k == KT - TC:
                h2_there()
            scores(0, k)
            if k in T_AT:
                t_product(1, T_AT.index(k))
            if k == 12:
                transpose_h2()
        transpose_max(0)
        spread_max(0)
        chunk(0, first=True)
        with pe.Fori(1, NC - 2) as c:
            chunk(c)
        chunk(NC - 2, more2=False)
        chunk(NC - 1, more=False, more2=False)
        for t in range(TC):
            transpose_o(NC - 1, t, TAIL_PS[t])
        for t in range(TC):
            project(NC - 1, t, TAIL_PS[t])

    return sync, pool, vector, scalar, tensor


_INS = ["x", "adj", "L0_gnn_W1", "L0_gnn_b1", "L0_gnn_W2", "L0_gnn_b2", "L1_gnn_Wq", "L1_gnn_Wk", "L1_gnn_Wv"]


def kernel(**inputs):
    import numpy as _np
    import concourse.bacc as _bacc
    from concourse import mybir as _mybir
    from concourse.bass_utils import run_bass_kernel_spmd as _run

    nc = _bacc.Bacc("TRN2", target_bir_lowering=False, num_devices=1)
    arrays, args = {}, []
    for name in _INS:
        a = _np.ascontiguousarray(inputs[name])
        if a.dtype == _np.bool_:
            a = a.view(_np.uint32)
        arrays[f"in_{name}"] = a
        args.append(nc.dram_tensor(f"in_{name}", a.shape, _mybir.dt.from_np(a.dtype), kind="ExternalInput").ap())
    out = nc.dram_tensor("out_x", (4096, 256), _mybir.dt.float32, kind="ExternalOutput").ap()
    args[1] = args[1].bitcast(_mybir.dt.uint8)
    build(nc, *args, out)
    r = _run(nc, [arrays], core_ids=[0])
    return r.results[0]["out_x"]
```

```python
import math
from contextlib import ExitStack
import concourse.bass as bass
from concourse import mybir

F32, F16, U8 = mybir.dt.float32, mybir.dt.float16, mybir.dt.uint8
I32, U32 = mybir.dt.int32, mybir.dt.uint32
ALU, ACT, AX = mybir.AluOpType, mybir.ActivationFunctionType, mybir.AxisListType

P = 128
N, D, HID = 4096, 256, 512
CH = 512
NC = N // CH
KT = N // P
TC = CH // P
DH = D // P
HB = HID // P
GR = 4
GW = N // GR
NW = GW // 128
NEIGH = 16
PAIRS = N // 2
EPS = 1e-5
SCAN_AT = [2, 5, 7, 16]
TR_H2_AT = [20, 23]
EARLY = 2
FIRST_SCAN_AT = [12, 16, 22, 28]
H_SCALE = 2048.0
P_SCALE = 16384.0
NEG = -1.0e30
NEG_FLOOR = -5.0e29
TINY = 1e-30
ST_RING, X_RING, QK_RING = 8, 8, 2
AHEAD = 2
LAG = 4
V_W = D + 2


class Chain:

    def __init__(self, engine, sem, per):
        self.engine, self.sem, self.per = engine, sem, per

    def begin(self, chunk):
        self.chunk, self.n = chunk, 0

    def then(self, instruction):
        instruction.then_inc(self.sem, 1)
        self.n += 1
        self.engine.wait_ge(self.sem, self.chunk * self.per + self.n)

    def end(self):
        assert self.n == self.per, (self.n, self.per)


def build(nc, x, adj, w1, b1, w2, b2, wq, wk, wv, out):
    x2_dram = nc.dram_tensor("x2_scratch", (N, D), F32, kind="Internal").ap()
    h_dram = nc.dram_tensor("h_scratch", (N, 2 * D), F16, kind="Internal").ap()
    with ExitStack() as ctx:
        mem = Memory(nc, ctx)
        sync0, pool0, vector0, scalar0, tensor0 = layer0(nc, mem, x, adj, w1, b1, w2, b2, wq, wk, wv, h_dram, x2_dram)
        sync1, pool1, vector1, scalar1, tensor1 = layer1(nc, mem, adj, x2_dram, out)
        block = ctx.enter_context(nc.Block())

        @block.sync
        def _(sp):
            sync1(sp, sync0(sp))

        @block.gpsimd
        def _(pool):
            pool0(pool)
            pool1(pool)

        @block.vector
        def _(dve):
            vector1(dve, vector0(dve))

        @block.scalar
        def _(act):
            scalar1(act, scalar0(act))

        @block.tensor
        def _(pe):
            tensor1(pe, tensor0(pe))


class Memory:

    BIG, SMALL = 64 * 1024, 52 * 1024

    def __init__(self, nc, ctx):
        self.nc, self.ctx = nc, ctx
        self.h2t = self.sb("h2t", [P, DH, 2, N], F16)
        self.v_hi = self.sb("v_hi", [P, KT, V_W], F16)
        self.v_lo = self.sb("v_lo", [P, KT, D], F16)
        self.ident = self.sb("ident", [P, P], F32)
        self.ones = self.sb("ones", [P, P], F32)
        self.ident16 = self.sb("ident16", [P, P], F16)
        self.a_sp = self.sb("a_sp", [P, DH, 2, D], F16)
        self.exp_scale = self.sb("exp_scale", [P, 1], F32)
        self.wvt = self.sb("wvt", [P, DH, D], F32)
        self.big = self.sb("big", [P, self.BIG], U8)
        self.small = self.sb("small", [P, self.SMALL], U8)
        self.adj_pair = self.sb("adj_pair", [P, 2, N], U8)
        self.rows_a = self.sb("rows_a", [P, TC, D], F32)
        self.rows_b = self.sb("rows_b", [P, TC, D], F32)
        self.rows_c = self.sb("rows_c", [P, TC, D], F32)
        self.banks = ctx.enter_context(nc.psum_tensor("banks", [P, 8, CH], F32))

    def sb(self, name, shape, dt):
        return self.ctx.enter_context(self.nc.sbuf_tensor(name, shape, dt))

    def sem(self, name):
        return self.ctx.enter_context(self.nc.semaphore(name))


class Cut:

    def __init__(self, place):
        self.place, self.at = place, 0

    def __call__(self, shape, dt):
        size = {F32: 4, F16: 2, U8: 1, mybir.dt.int8: 1}[dt] * math.prod(shape)
        part = self.place[:, self.at:self.at + size].bitcast(dt)
        self.at += size
        names = "abcd"[:len(shape)]
        return part.rearrange(f"p ({' '.join(names)}) -> p {' '.join(names)}",
                              **dict(zip(names[1:], shape[1:]))) if len(shape) > 1 else part


def layer0(nc, mem, x, adj, w1, b1, w2, b2, wq, wk, wv, h_dram, x2_dram):
    sb, sem = mem.sb, mem.sem
    ident, ones, ident16 = mem.ident, mem.ones, mem.ident16
    h2t, v_hi, v_lo = mem.h2t, mem.v_hi, mem.v_lo
    a_sp, exp_scale, wvt = mem.a_sp, mem.exp_scale, mem.wvt
    cut = Cut(mem.big)
    h_j = cut([KT, 2, D], F16)
    adj_t = cut([NW, CH, 4], U8)
    adj_blk = cut([CH // 32, GW], U8)
    assert cut.at == mem.BIG
    cut = Cut(mem.small)
    st = cut([ST_RING, CH], F16)
    act_t = cut([HB, CH], F32)
    w1_sb = cut([DH, HID], F32)
    w2_sb = cut([HB, D], F32)
    cum = cut([2, PAIRS], F16)
    hid_t = cut([DH, CH], F32)
    h_nat = cut([TC, 2, D], F16)
    sign_out = cut([PAIRS], mybir.dt.int8)
    thr_diag = cut([TC, P], F32)
    thr_b = cut([CH], F32)
    h_16 = cut([2, D], F16)[0:NEIGH, :, :]
    fill_t = cut([CH], F16)[0:NEIGH, :]
    h2_st = cut([2, TC, D], F16)
    assert cut.at <= mem.SMALL
    adj_nat = mem.adj_pair
    x_in, x2_sb, h32 = mem.rows_a, mem.rows_b, mem.rows_c
    b1_sb = sb("b1_sb", [P, HB], F32)
    b2_b = sb("b2_b", [P, D], F32)
    sixteen_i = sb("sixteen_i", [P, P], F16)
    j_col = sb("j_col", [P, KT], F32)
    half_col = sb("half_col", [P, 2], F32)
    acc = sb("acc", [P, TC, 2], F32)
    thr = sb("thr", [P, 3, TC], F32)
    fill_na = sb("fill_na", [P, TC, NEIGH], F16)
    fill_run = sb("fill_run", [P, TC, NEIGH], F16)
    fill_need = sb("fill_need", [P, TC], F32)
    sixteen = sb("sixteen", [P, 1], F32)
    pool_pad = sb("pool_pad", [P, 1], F32)
    fill = sb("fill", [P, TC, NEIGH], F16)
    stats = sb("stats", [P, TC, 6], F32)
    mv = sb("mv", [P, TC, 2], F32)
    rs = sb("rs", [P, TC, 2], F32)
    var = sb("var", [P, TC], F32)
    wait_pad = sb("wait_pad", [P, 1], F32)
    std = sb("std", [P, TC], F32)
    inv = sb("inv", [P, TC, 2], F32)
    x_all = h2t[:, :, :, :].rearrange("p h s n -> p (h s n)").bitcast(F32).rearrange("p (k m) -> p k m", k=KT)
    scratch = v_lo[:, :, :].rearrange("p k m -> p (k m)").bitcast(F32)

    def part(at, width):
        return scratch[:, at * KT:(at + width) * KT].rearrange("p (t n) -> p t n", n=width)
    ln1_set = (part(0, 6), part(6, 2), part(8, 1)[:, :, 0], part(9, 1)[:, :, 0], part(10, 2), part(12, 2))
    ln2_set = (stats, mv, var[:, :], std[:, :], inv, rs)
    wq_sb, wk_sb, wv_sb, a_f = (act_t[:, i, :].rearrange("p (h d) -> p h d", h=DH) for i in range(4))
    b2_sb = hid_t[0:1, 0, 0:D]
    j_int = hid_t[:, 1, 0:KT].bitcast(I32)
    a_abs = sb("a_abs", [P, 4], F32)
    sc = sb("sc", [1, 4], F32)
    res_ps = mem.banks[:, 0:2, :]
    hid_ps = mem.banks[:, 2:4, :]
    mlp_ps = mem.banks[:, 4:6, :].rearrange("p b (t d) -> p (b t) d", d=D)
    thr_ps = mem.banks[:, 6, :]
    tr_ps = mem.banks[:, 7, :].bitcast(F16).rearrange("p (s n) -> p s n", s=2)
    a_ps = mem.banks[:, 2, :].rearrange("p (h d) -> p h d", h=DH)
    wvt_ps = mem.banks[:, 3, :].rearrange("p (h d) -> p h d", h=DH)
    m_ps = mem.banks[:, 4, 0:P + 1]
    b2_ps = mem.banks[:, 5, 0:D]
    w_loaded = sem("mlp_weights_loaded")
    x_loaded = [sem(f"x_loaded{i}") for i in range(2)]
    qkv_loaded, shared_consts, zeroed = sem("qkv_loaded"), sem("shared_consts"), sem("zeroed")
    a_copied = sem("a_copied")
    a_done, wvt_done, b2_done, row_done, bc_done = sem("a_done"), sem("wvt_done"), sem("b2_done"), sem("row_done"), sem("bc_done")
    max_ready, scale_ready, setup_chain, setup_done, b2_ready = sem("a_max_ready"), sem("scale_ready"), sem("setup_chain"), sem("setup_done"), sem("b2_ready")
    xin_biased = sem("xin_biased")
    consts = sem("l0_consts")
    pool_chain = sem("l0_pool_chain")
    h_scaled, h_hi_done, h_lo_done, h_stored = sem("h_scaled"), sem("h_hi_done"), sem("h_lo_done"), sem("h_stored")
    h_relu, h16_loaded, ln_ready = sem("h_relu"), sem("h16_loaded"), sem("ln_ready")
    ln1_chain, prep_chain, ln2_chain = sem("ln1_chain"), sem("prep_chain"), sem("ln2_chain")
    nat_loaded = [sem(f"nat_loaded{i}") for i in range(2)]
    blk_loaded, scanned, transposed, counted = sem("blk_loaded"), sem("scanned"), sem("transposed"), sem("counted")
    tile_read, diag_ready, need_ready = sem("tile_read"), sem("diag_ready"), sem("need_ready")
    thr_done, fill_tr_done, thr_copied, fill_copied = sem("thr_done"), sem("fill_tr_done"), sem("thr_copied"), sem("fill_copied")
    st_ready, st_used, hnat_loaded, res_done = sem("st_ready"), sem("st_used"), sem("hnat_loaded"), sem("res_done")
    hid_in_ready, hid_done, act_ready, mlp_done = sem("hid_in_ready"), sem("hid_done"), sem("act_ready"), sem("mlp_done")
    xin_loaded, x2_added, x2_stored = sem("xin_loaded"), sem("x2_added"), sem("x2_stored")
    std1_done, std2_done, var2_ready = sem("std1_done"), sem("std2_done"), sem("var2_ready")
    ln2_ready, h2_relu, h2_hi, h2_lo = sem("ln2_ready"), sem("h2_relu"), sem("h2_hi"), sem("h2_lo")
    h2_tr, h2_copied, v_stored = sem("h2_tr"), sem("h2_copied"), sem("v_stored")

    def rows(t, c):
        return t[bass.ds(c * CH, CH), :].rearrange("(t p) m -> p t m", p=P)

    def sync(sp):
        def load_nat(c, t):
            n = c * TC + t
            if not (isinstance(c, int) and n < 2):
                sp.wait_ge(scanned, n - 1)
                sp.wait_ge(tile_read, n - 1)
            sp.dma_start(adj_nat[:, t % 2, :], adj[bass.ds(c * CH + t * P, P), :]).then_inc(nat_loaded[t % 2], 16)

        def load_blk(c):
            if not (isinstance(c, int) and c == 0):
                sp.wait_ge(transposed, c)
            for g in range(GR):
                src = adj[bass.ds(c * CH, CH), g * GW:(g + 1) * GW].rearrange("(i c) m -> c i m", c=32)
                sp.dma_start(adj_blk[32 * g:32 * (g + 1), :, :], src).then_inc(blk_loaded, 16)

        load_nat(0, 0)
        load_nat(0, 1)
        HW = NW // 2

        def in_k_order(t, half, g, m):
            return t[g * GW + half * HW * P:g * GW + (half + 1) * HW * P, :]\
                .rearrange("(w r b) m -> r w (b m)", r=32, b=4)

        for half in range(2):
            for g in range(GR):
                sp.dma_start(x_all[32 * g:32 * (g + 1), 16 * half:16 * (half + 1), :]
                             .rearrange("p (w b) m -> p w (b m)", b=4), in_k_order(x, half, g, D))\
                    .then_inc(x_loaded[half], 16)
            if half == 0:
                load_nat(0, 2)
                load_nat(0, 3)
        load_blk(0)
        for dst, src in ((wq_sb, wq), (wk_sb, wk), (wv_sb, wv)):
            sp.dma_start(dst, src.rearrange("(o p) d -> p o d", p=P)).then_inc(qkv_loaded, 16)
        sp.dma_start(b1_sb[:, :], b1.rearrange("(o p) -> p o", p=P), allow_slow_non_contiguous=True).then_inc(w_loaded, 16)
        sp.dma_start(b2_sb, b2.rearrange("(a n) -> a n", a=1)).then_inc(w_loaded, 16)
        sp.dma_start(w1_sb, w1.rearrange("(o p) n -> p o n", p=P)).then_inc(w_loaded, 16)
        sp.dma_start(w2_sb, w2.rearrange("(o p) n -> p o n", p=P)).then_inc(w_loaded, 16)
        load_nat(1, 0)
        load_nat(1, 1)
        load_blk(1)

        def store_h(half):
            sp.wait_ge(h_hi_done, HW * (half + 1))
            sp.wait_ge(h_lo_done, HW * (half + 1))
            for g in range(GR):
                sp.dma_start(in_k_order(h_dram, half, g, 2 * D), h_j[32 * g:32 * (g + 1), 16 * half:16 * (half + 1), :, :]
                             .rearrange("p (w b) s m -> p w (b s m)", b=4)).then_inc(h_stored, 16)

        store_h(0)
        load_nat(1, 2)
        load_nat(1, 3)
        sp.wait_ge(h_stored, 16 * GR)
        sp.dma_start(h_16, h_dram[0:NEIGH, :].rearrange("p (s m) -> p s m", s=2)).then_inc(h16_loaded, 16)

        def chunk(c, first=False, more=True, more2=True):
            if not first:
                sp.wait_ge(res_done, c)
            sp.dma_start(h_nat[:, :, :, :], h_dram[bass.ds(c * CH, CH), :]
                         .rearrange("(t p) (s m) -> p t s m", p=P, s=2)).then_inc(hnat_loaded, 16)
            if first:
                store_h(1)
            if more and not first:
                load_nat(c + 1, 2)
                load_nat(c + 1, 3)
            if more2:
                load_nat(c + 2, 0)
            if not first:
                finish_rows(c - 1)
            sp.dma_start(x_in[:, :, :], rows(x, c)).then_inc(xin_loaded, 16)
            if not first:
                store_values(c - 1)
            if more2:
                load_nat(c + 2, 1)
                load_blk(c + 2)

        def finish_rows(c):
            sp.wait_ge(x2_added, c + 1)
            sp.dma_start(rows(x2_dram, c), x2_sb[:, :, :]).then_inc(x2_stored, 16)

        def store_values(c):
            sp.wait_ge(h2_hi, c + 1)
            sp.wait_ge(h2_lo, c + 1)
            sp.dma_start(v_hi[:, bass.ds(c * TC, TC), 0:D], h2_st[:, 0, :, :]).then_inc(v_stored, 16)
            sp.dma_start(v_lo[:, bass.ds(c * TC, TC), :], h2_st[:, 1, :, :]).then_inc(v_stored, 16)

        chunk(0, first=True)
        sp.wait_ge(h_stored, 16 * GR * 2)
        with sp.Fori(1, NC - 2) as c:
            chunk(c)
        chunk(NC - 2, more2=False)
        chunk(NC - 1, more=False, more2=False)


        def adjacency_read():
            sp.wait_ge(scanned, TC * NC)
            sp.wait_ge(tile_read, TC * NC)

        def values_stored():
            store_values(NC - 1)
            sp.wait_ge(x2_stored, 16 * NC)
            sp.wait_ge(v_stored, 32 * NC)

        return adjacency_read, (lambda: finish_rows(NC - 1)), values_stored

    def pool(pool):
        nc.gpsimd.memset(ident[:, :], 0.0).then_inc(zeroed, 1)
        nc.gpsimd.memset(ident16[:, :], 0.0).then_inc(zeroed, 1)
        nc.gpsimd.memset(ones[:, :], 1.0).then_inc(shared_consts, 1)
        nc.gpsimd.memset(v_hi[:, :, D:V_W], 1.0).then_inc(shared_consts, 1)
        pool.wait_ge(zeroed, 2)
        for m in (ident, ident16):
            nc.gpsimd.affine_select(out=m[:, :], in_=m[:, :], compare_op=ALU.not_equal, fill=1.0,
                                    base=0, pattern=[[-1, P]], channel_multiplier=1).then_inc(shared_consts, 1)
        nc.gpsimd.iota(j_int, pattern=[[P, NW], [1, 4]], base=0, channel_multiplier=4).then_inc(consts, 1)
        nc.gpsimd.memset(half_col[:, 0:1], NEIGH - 0.5).then_inc(consts, 1)
        nc.gpsimd.memset(half_col[:, 1:2], NEIGH + 0.5).then_inc(consts, 1)
        nc.gpsimd.memset(sixteen[:, :], float(NEIGH)).then_inc(consts, 1)
        nc.gpsimd.memset(fill_run[:, :, :], 1.0).then_inc(pool_chain, 1)
        pool.wait_ge(pool_chain, 1)
        nc.gpsimd.memset(fill_run[:, :, 0:1], 0.0).then_inc(consts, 1)
        nc.gpsimd.memset(sixteen_i[:, :], 0.0).then_inc(pool_chain, 1)
        pool.wait_ge(pool_chain, 2)
        nc.gpsimd.affine_select(out=sixteen_i[:, :], in_=sixteen_i[:, :], compare_op=ALU.not_equal,
                                fill=float(NEIGH), base=0, pattern=[[-1, P]], channel_multiplier=1)\
            .then_inc(consts, 1)

        def falses(c, t):
            pool.wait_ge(nat_loaded[t % 2], 16 * (c * 2 + t // 2 + 1))
            if t == 0 and not (isinstance(c, int) and c == 0):
                pool.wait_ge(diag_ready, c)
            if not (isinstance(c, int) and c == 0 and t == 0):
                pool.wait_ge(tile_read, TC * c + t)
            nc.gpsimd.tensor_tensor(pool_pad[:, :], sixteen[:, :], sixteen[:, :], ALU.subtract)
            nc.gpsimd.tensor_copy(fill_na[:, t, :], adj_nat[:, t % 2, 0:NEIGH]).then_inc(tile_read, 1)

        def need(c, t):
            pool.wait_ge(scanned, TC * c + t + 1)
            nc.gpsimd.tensor_tensor(fill_need[:, t:t + 1], sixteen[:, :], cum[:, t % 2, PAIRS - 1:PAIRS],
                                    ALU.subtract).then_inc(need_ready, 1)

        def ln2_low(c):
            pool.wait_ge(h2_hi, c + 1)
            if not (isinstance(c, int) and c == 0):
                pool.wait_ge(v_stored, 32 * c)
                pool.wait_ge(h2_tr, 2 * c)
            nc.gpsimd.tensor_tensor(h2_st[:, 1, :, :], h32[:, :, :], h2_st[:, 0, :, :], ALU.subtract)\
                .then_inc(h2_lo, 1)

        def bias_rows(c):
            pool.wait_ge(xin_loaded, 16 * (c + 1))
            for t in range(TC):
                nc.gpsimd.tensor_tensor(x_in[:, t, :], x_in[:, t, :], b2_b[:, :], ALU.add).then_inc(xin_biased, 1)

        def h_low(w):
            k = slice(4 * w, 4 * (w + 1))
            pool.wait_ge(h_hi_done, w + 1)
            nc.gpsimd.tensor_tensor(h_j[:, k, 1, :], x_all[:, k, :], h_j[:, k, 0, :], ALU.subtract)\
                .then_inc(h_lo_done, 1)

        def chunk(c, more=True):
            if more:
                for t in range(TC - 1):
                    falses(c + 1, t)
                    need(c + 1, t)
            bias_rows(c)
            if more:
                falses(c + 1, TC - 1)
            ln2_low(c - 1)
            if more:
                need(c + 1, TC - 1)

        pool.wait_ge(shared_consts, 4)
        pool.wait_ge(consts, 6)
        for t in range(TC):
            falses(0, t)
            need(0, t)
        for w in range(NW):
            h_low(w)
            if w == 4:
                falses(1, 0)
            if w == 5:
                need(1, 0)
                falses(1, 1)
        need(1, 1)
        falses(1, 2)
        need(1, 2)
        pool.wait_ge(b2_ready, 1)
        bias_rows(0)
        falses(1, 3)
        need(1, 3)
        with pool.Fori(1, NC - 1) as c:
            chunk(c)
        chunk(NC - 1, more=False)
        ln2_low(NC - 1)

    def vector(dve):
        ln1 = Chain(dve, ln1_chain, 6)
        prep = Chain(dve, prep_chain, 6)
        ln2 = Chain(dve, ln2_chain, 6)

        def row_stats(src, stats, tiles):
            for t in tiles:
                last = nc.vector.bn_stats(stats[:, t, :], src[:, t, :])
            return last

        def row_var(last, chain, ready, at, tiles):
            stats, mv, var = at[0:3]
            chain.then(last)
            nc.vector.memset(wait_pad[:, :], 0.0)
            for t in range(tiles):
                last = nc.vector.bn_aggr(mv[:, t, :], stats[:, t, :])
            chain.then(last)
            nc.vector.tensor_single_scalar(var, mv[:, :, 1], EPS, ALU.add).then_inc(ready, 1)

        def row_scale(chain, done, before, at):
            mv, var, std, inv, rs = at[1:]
            dve.wait_ge(done, before)
            chain.then(nc.vector.reciprocal(inv[:, :, 0], std))
            chain.then(nc.vector.tensor_tensor(inv[:, :, 1], inv[:, :, 0], inv[:, :, 0], ALU.mult))
            chain.then(nc.vector.scalar_tensor_tensor(inv[:, :, 1], inv[:, :, 1], -0.5 * H_SCALE, var,
                                                      ALU.mult, ALU.mult))
            chain.then(nc.vector.scalar_tensor_tensor(rs[:, :, 0], inv[:, :, 1], 1.5 * H_SCALE, inv[:, :, 0],
                                                      ALU.add, ALU.mult))
            return nc.vector.scalar_tensor_tensor(rs[:, :, 1], mv[:, :, 0], -1.0, rs[:, :, 0],
                                                  ALU.mult, ALU.mult)

        def scan_tile(c, t):
            n = c * TC + t
            dve.wait_ge(nat_loaded[t % 2], 16 * (c * 2 + t // 2 + 1))
            if not (isinstance(c, int) and n < 2):
                dve.wait_ge(counted, 2 * (n - 1))
                dve.wait_ge(need_ready, n - 1)
            pairs = adj_nat[:, t % 2, :].rearrange("p (n b) -> p n b", b=2)
            nc.vector.tensor_tensor_scan(cum[:, t % 2, :], pairs[:, :, 0], pairs[:, :, 1], 0.0,
                                         ALU.add, ALU.add).then_inc(scanned, 1)

        def transpose_chunk(c):
            dve.wait_ge(blk_loaded, 16 * GR * (c + 1))
            if not (isinstance(c, int) and c == 0):
                dve.wait_ge(st_ready, KT * c)
            src = adj_blk[:, :, :].bitcast(U32)
            dst = adj_t[:, :, :, :].rearrange("p w i b -> p (w i b)").bitcast(U32)\
                .rearrange("p (w i) -> p w i", w=NW)
            for i in range(CH // 32):
                last = nc.vector.transpose(dst[:, :, 32 * i:32 * (i + 1)],
                                           src[:, i, :].rearrange("p (w r) -> p w r", w=NW))
            last.then_inc(transposed, 1)
            dve.wait_ge(transposed, c + 1)

        def thresholds(c):
            prep.begin(c)
            dve.wait_ge(need_ready, TC * (c + 1))
            if not (isinstance(c, int) and c == 0):
                dve.wait_ge(fill_tr_done, c)
            dve.wait_ge(tile_read, TC * (c + 1))
            prep.then(nc.vector.tensor_scalar(fill_na[:, :, :], fill_na[:, :, :], -1.0, 1.0, ALU.mult, ALU.add))
            prep.then(nc.vector.tensor_tensor_scan(fill[:, :, :].rearrange("p t n -> p (t n)"),
                                                   fill_run[:, :, :].rearrange("p t n -> p (t n)"),
                                                   fill_na[:, :, :].rearrange("p t n -> p (t n)"), 0.0,
                                                   ALU.mult, ALU.add))
            prep.then(nc.vector.tensor_tensor(fill[:, :, :], fill[:, :, :],
                                              fill_need[:, :].unsqueeze(2).broadcast_to([P, TC, NEIGH]), ALU.is_le))
            nc.vector.tensor_tensor(fill[:, :, :], fill[:, :, :], fill_na[:, :, :], ALU.mult)
            dve.wait_ge(counted, 2 * TC * (c + 1))
            prep.then(nc.vector.tensor_tensor(thr[:, 0, :], acc[:, :, 1], acc[:, :, 0], ALU.subtract))
            prep.then(nc.vector.tensor_scalar(thr[:, 1, :], thr[:, 0, :], 0.5, 1.0, ALU.mult, ALU.min))
            prep.then(nc.vector.scalar_tensor_tensor(thr[:, 2, :], acc[:, :, 0], float(PAIRS), thr[:, 1, :],
                                                     ALU.add, ALU.add))
            for t in range(TC):
                last = nc.vector.tensor_scalar(thr_diag[:, t, :], ident[:, :], thr[:, 2, t:t + 1], None, ALU.mult)
            last.then_inc(diag_ready, 1)
            prep.end()

        def select_tile(c, k):
            if not (isinstance(c, int) and c == 0 and k < ST_RING):
                dve.wait_ge(st_used, c * KT + k - ST_RING + 1)
            nc.vector.scalar_tensor_tensor(st[:, k % ST_RING, :], thr_b[:, :], j_col[:, k:k + 1],
                                           adj_t[:, k // 4, :, k % 4], ALU.is_ge, ALU.mult)\
                .then_inc(st_ready, 1)

        def ln2_stats(c):
            ln2.begin(c)
            dve.wait_ge(mlp_done, c + 1)
            dve.wait_ge(xin_biased, TC * (c + 1))
            if not (isinstance(c, int) and c == 0):
                dve.wait_ge(x2_stored, 16 * c)
            nc.vector.tensor_tensor(x2_sb[:, :, :], mlp_ps[:, :, :], x_in[:, :, :], ALU.add).then_inc(x2_added, 1)
            dve.wait_ge(x2_added, c + 1)
            if not (isinstance(c, int) and c == 0):
                dve.wait_ge(h2_relu, TC * c)
            row_var(row_stats(x2_sb, stats, range(TC)), ln2, var2_ready, ln2_set, TC)

        def ln2_scale(c):
            row_scale(ln2, std2_done, c + 1, ln2_set).then_inc(ln2_ready, 1)
            ln2.end()

        dve.wait_ge(consts, 6)
        for g in range(GR):
            last = nc.vector.tensor_single_scalar(j_col[32 * g:32 * (g + 1), :], j_int[32 * g:32 * (g + 1)],
                                                  float((GW - P) * g), ALU.add)
        last.then_inc(consts, 1)
        def chunk(c, first=False, more=True):
            dve.wait_ge(thr_copied, c + 1)
            scans = FIRST_SCAN_AT if first else SCAN_AT
            for k in range(KT):
                select_tile(c, k)
                if more and k in scans:
                    scan_tile(c + 1, scans.index(k))
                if not first and k == 9:
                    ln2_stats(c - 1)
                if not first and k == 12:
                    ln2_scale(c - 1)
                if first and k == 14:
                    setup_max()
                if first and k == 23:
                    setup_scale()
                if first and k == 30:
                    setup_split()
            if more:
                thresholds(c + 1)
                transpose_chunk(c + 1)

        setup = Chain(dve, setup_chain, 7)
        setup.begin(0)

        def setup_max():
            dve.wait_ge(a_copied, 1)
            nc.vector.tensor_reduce(out=a_abs[:, 0:1], in_=a_f, axis=AX.XY, op=ALU.max,
                                    apply_absolute_value=True).then_inc(max_ready, 1)

        def setup_scale():
            dve.wait_ge(row_done, 1)
            setup.then(nc.vector.tensor_reduce(out=sc[0:1, 0:1], in_=m_ps[0:1, 0:P], axis=AX.X, op=ALU.max))
            setup.then(nc.vector.tensor_scalar(sc[0:1, 0:1], sc[0:1, 0:1], 2.0 ** -40, 1.0 / 128, ALU.max, ALU.mult))
            setup.then(nc.vector.reciprocal(sc[0:1, 1:2], sc[0:1, 0:1]))
            nc.vector.tensor_single_scalar(sc[0:1, 2:3].bitcast(U32), sc[0:1, 1:2].bitcast(U32), 0x7F800000,
                                           ALU.bitwise_and).then_inc(scale_ready, 1)

        def setup_split():
            dve.wait_ge(bc_done, 1)
            setup.then(nc.vector.tensor_copy(a_abs[:, 2:3], m_ps[:, P:P + 1]))
            setup.then(nc.vector.tensor_single_scalar(a_abs[:, 3:4], a_abs[:, 2:3], H_SCALE, ALU.mult))
            setup.then(nc.vector.reciprocal(exp_scale[:, :], a_abs[:, 3:4]))
            setup.then(nc.vector.tensor_scalar(a_sp[:, :, 0, :], a_f, a_abs[:, 2:3], None, ALU.mult))
            nc.vector.scalar_tensor_tensor(a_sp[:, :, 1, :], a_f, a_abs[:, 2:3], a_sp[:, :, 0, :],
                                           ALU.mult, ALU.subtract).then_inc(setup_done, 1)
            setup.end()

        dve.wait_ge(shared_consts, 4)
        scan_tile(0, 0)
        scan_tile(0, 1)
        ln1.begin(0)
        for half in range(2):
            dve.wait_ge(x_loaded[half], 16 * GR)
            last = row_stats(x_all, ln1_set[0], range(16 * half, 16 * (half + 1)))
            if half == 0:
                scan_tile(0, 2)
                scan_tile(0, 3)
        row_var(last, ln1, ln_ready, ln1_set, KT)
        thresholds(0)
        row_scale(ln1, std1_done, 1, ln1_set).then_inc(h_scaled, 1)
        ln1.end()
        transpose_chunk(0)
        chunk(0, first=True)
        with dve.Fori(1, NC - 1) as c:
            chunk(c)
        chunk(NC - 1, more=False)
        return (lambda: ln2_stats(NC - 1)), (lambda: ln2_scale(NC - 1))

    def scalar(act):
        def relu_rows(src, done):
            for t in range(TC):
                nc.scalar.activation(h32[:, t, :], src[:, t, :], ACT.Relu, bias=rs[:, t, 1:2],
                                     scale=rs[:, t, 0:1]).then_inc(done, 1)

        def count_tile(c, t):
            act.wait_ge(scanned, c * TC + t + 1)
            if t == 0 and not (isinstance(c, int) and c == 0):
                act.wait_ge(diag_ready, c)
            for s in range(2):
                n = 2 * (c * TC + t) + s
                if not (isinstance(c, int) and n == 0):
                    act.wait_ge(counted, n)
                nc.scalar.activation(sign_out[:, :], cum[:, t % 2, :], ACT.Sign, bias=half_col[:, s:s + 1],
                                     scale=-1.0, accum_out=acc[:, t, s:s + 1]).then_inc(counted, 1)

        def copy_prep(c):
            act.wait_ge(thr_done, c + 1)
            nc.scalar.activation(thr_b[:, :], thr_ps[:, :], ACT.Copy).then_inc(thr_copied, 1)
            act.wait_ge(fill_tr_done, c + 1)
            nc.scalar.activation(fill_t[:, :], tr_ps[0:NEIGH, 0, :], ACT.Copy).then_inc(fill_copied, 1)

        def ln2_std(c):
            act.wait_ge(var2_ready, c + 1)
            nc.scalar.activation(std[:, :], var[:, :], ACT.Sqrt).then_inc(std2_done, 1)

        def ln2_rows(c):
            act.wait_ge(ln2_ready, c + 1)
            if not (isinstance(c, int) and c == 0):
                act.wait_ge(h2_lo, c)
            relu_rows(x2_sb, h2_relu)
            act.wait_ge(h2_relu, TC * (c + 1))
            if not (isinstance(c, int) and c == 0):
                act.wait_ge(v_stored, 32 * c)
                act.wait_ge(h2_tr, 2 * c)
            nc.scalar.activation(h2_st[:, 0, :, :], h32[:, :, :], ACT.Copy).then_inc(h2_hi, 1)

        def copy_h2t(c):
            for h in range(DH):
                act.wait_ge(h2_tr, DH * c + h + 1)
                nc.scalar.activation(h2t[:, h, :, bass.ds(c * CH, CH)], tr_ps[:, :, :], ACT.Copy)\
                    .then_inc(h2_copied, 1)

        def mlp_in(c):
            act.wait_ge(res_done, c + 1)
            if not (isinstance(c, int) and c == 0):
                act.wait_ge(hid_done, HB * c)
            nc.scalar.activation(hid_t[:, :, :], res_ps[:, :, :], ACT.Copy, scale=1.0 / (NEIGH * H_SCALE))\
                .then_inc(hid_in_ready, 1)

        def mlp_relu(c):
            for b in range(HB):
                act.wait_ge(hid_done, HB * c + b + 1)
                if b == 0 and not (isinstance(c, int) and c == 0):
                    act.wait_ge(mlp_done, c)
                nc.scalar.activation(act_t[:, b, :], hid_ps[:, b % 2, :], ACT.Relu, bias=b1_sb[:, b:b + 1])\
                    .then_inc(act_ready, 1)

        act.wait_ge(consts, 6)
        for t in range(TC):
            count_tile(0, t)
        act.wait_ge(ln_ready, 1)
        nc.scalar.activation(ln1_set[3], ln1_set[2], ACT.Sqrt).then_inc(std1_done, 1)
        act.wait_ge(h_scaled, 1)
        for k in range(KT):
            nc.scalar.activation(x_all[:, k, :], x_all[:, k, :], ACT.Relu, bias=ln1_set[5][:, k, 1:2],
                                 scale=ln1_set[5][:, k, 0:1]).then_inc(h_relu, 1)
            if k % 4 == 3:
                w = k // 4
                act.wait_ge(h_relu, k + 1)
                nc.scalar.activation(h_j[:, 4 * w:4 * (w + 1), 0, :], x_all[:, 4 * w:4 * (w + 1), :], ACT.Copy)\
                    .then_inc(h_hi_done, 1)
            if k == 3:
                copy_prep(0)
            if k == 23:
                count_tile(1, 0)
            if k == 11:
                act.wait_ge(a_done, 1)
                nc.scalar.activation(a_f, a_ps, ACT.Copy).then_inc(a_copied, 1)
                act.wait_ge(wvt_done, 1)
                nc.scalar.activation(wvt[:, :, :], wvt_ps, ACT.Copy, scale=1.0 / H_SCALE).then_inc(setup_done, 1)
        act.wait_ge(b2_done, 1)
        nc.scalar.activation(b2_b[:, :], b2_ps, ACT.Copy).then_inc(b2_ready, 1)
        act.wait_ge(w_loaded, 64)

        def chunk(c, first=False, more=True):
            if more:
                for t in range(1 if first else 0, TC - 1):
                    count_tile(c + 1, t)
            if not first:
                ln2_std(c - 1)
                ln2_rows(c - 1)
            if more:
                count_tile(c + 1, TC - 1)
            if not first:
                copy_h2t(c - 1)
            mlp_in(c)
            if more:
                copy_prep(c + 1)
                mlp_relu(c)

        chunk(0, first=True)
        with act.Fori(1, NC - 1) as c:
            chunk(c)
        chunk(NC - 1, more=False)
        return [lambda step=step: step(NC - 1) for step in (mlp_relu, ln2_std, ln2_rows, copy_h2t)]

    def tensor(pe):
        def prep_chunk(c):
            pe.wait_ge(diag_ready, c + 1)
            if not (isinstance(c, int) and c == 0):
                pe.wait_ge(thr_copied, c)
            for t in range(TC):
                last = nc.tensor.matmul(thr_ps[:, t * P:(t + 1) * P], ones[:, :], thr_diag[:, t, :],
                                        start=True, stop=True)
            last.then_inc(thr_done, 1)
            if not (isinstance(c, int) and c == 0):
                pe.wait_ge(fill_copied, c)
            if not (isinstance(c, int) and c < 2):
                pe.wait_ge(h2_copied, DH * (c - 1))
            for t in range(TC):
                last = nc.tensor.transpose(tr_ps[0:NEIGH, 0, t * P:(t + 1) * P], fill[:, t, :], ident16[:, :])
            last.then_inc(fill_tr_done, 1)

        def gather_tile(c, k):
            if isinstance(c, int) and c == 0 and k % 4 == 0:
                pe.wait_ge(h_lo_done, k // 4 + 1)
            pe.wait_ge(st_ready, c * KT + k + 1)
            for h in range(DH):
                for s in range(2):
                    last = nc.tensor.matmul(res_ps[:, h, :], h_j[:, k, s, h * P:(h + 1) * P],
                                            st[:, k % ST_RING, :], start=(k == 0 and s == 0), stop=False)
            last.then_inc(st_used, 1)

        def gather_rest(c):
            if isinstance(c, int) and c == 0:
                pe.wait_ge(h16_loaded, 16)
            pe.wait_ge(fill_copied, c + 1)
            for h in range(DH):
                for s in range(2):
                    nc.tensor.matmul(res_ps[:, h, :], h_16[:, s, h * P:(h + 1) * P], fill_t[:, :],
                                     start=False, stop=False)
            pe.wait_ge(hnat_loaded, 16 * (c + 1))
            for h in range(DH):
                for t in range(TC):
                    for s in range(2):
                        last = nc.tensor.matmul(res_ps[:, h, t * P:(t + 1) * P], h_nat[:, t, s, h * P:(h + 1) * P],
                                                sixteen_i[:, :], start=False,
                                                stop=(t == TC - 1 and s == 1))
            last.then_inc(res_done, 1)

        def mlp_up(c):
            if isinstance(c, int) and c == 0:
                pe.wait_ge(setup_done, 2)
            pe.wait_ge(hid_in_ready, c + 1)
            for b in range(HB):
                if not (isinstance(c, int) and c == 0 and b < 2):
                    pe.wait_ge(act_ready, HB * c + b - 1)
                for h in range(DH):
                    last = nc.tensor.matmul(hid_ps[:, b % 2, :], w1_sb[:, h, b * P:(b + 1) * P], hid_t[:, h, :],
                                            start=(h == 0), stop=(h == DH - 1))
                last.then_inc(hid_done, 1)

        def mlp_down(c):
            if not (isinstance(c, int) and c == 0):
                pe.wait_ge(x2_added, c)
            pe.wait_ge(act_ready, HB * (c + 1))
            for t in range(TC):
                for b in range(HB):
                    last = nc.tensor.matmul(mlp_ps[:, t, :], act_t[:, b, t * P:(t + 1) * P], w2_sb[:, b, :],
                                            start=(b == 0), stop=(b == HB - 1))
            last.then_inc(mlp_done, 1)

        def transpose_h2(c, halves=range(DH)):
            for h in halves:
                for s, ready in enumerate((h2_hi, h2_lo)):
                    if h == 0:
                        pe.wait_ge(ready, c + 1)
                        if s == 0:
                            if not (isinstance(c, int) and c == 0):
                                pe.wait_ge(h2_copied, DH * c)
                            pe.wait_ge(fill_copied, c + 2 if not last_chunk(c) else NC)
                    elif s == 0:
                        pe.wait_ge(h2_copied, DH * c + h)
                    for t in range(TC):
                        last = nc.tensor.transpose(tr_ps[:, s, t * P:(t + 1) * P],
                                                   h2_st[:, s, t, h * P:(h + 1) * P], ident16[:, :])
                last.then_inc(h2_tr, 1)

        def last_chunk(c):
            return isinstance(c, int) and c == NC - 1

        def chunk(c):
            for k in range(EARLY, KT):
                gather_tile(c, k)
                if k in TR_H2_AT:
                    transpose_h2(c - 1, [TR_H2_AT.index(k)])
            gather_rest(c)
            prep_chunk(c + 1)
            mlp(c)

        def mlp(c):
            mlp_up(c)
            for k in range(EARLY):
                gather_tile(c + 1, k)
            mlp_down(c)

        def weights_1():
            pe.wait_ge(w_loaded, 64)
            nc.tensor.matmul(b2_ps, ones[0:1, :], b2_sb, start=True, stop=True).then_inc(b2_done, 1)
            pe.wait_ge(qkv_loaded, 48)
            for h in range(DH):
                for o in range(DH):
                    last = nc.tensor.matmul(a_ps[:, h, :], wq_sb[:, o, h * P:(h + 1) * P], wk_sb[:, o, :],
                                            start=(o == 0), stop=(o == DH - 1))
            last.then_inc(a_done, 1)
            for h in range(DH):
                for o in range(DH):
                    last = nc.tensor.transpose(wvt_ps[:, h, o * P:(o + 1) * P], wv_sb[:, o, h * P:(h + 1) * P],
                                               ident[:, :])
            last.then_inc(wvt_done, 1)

        pe.wait_ge(shared_consts, 4)
        pe.wait_ge(consts, 6)
        prep_chunk(0)
        weights_1()
        for k in range(KT):
            gather_tile(0, k)
            if k == 15:
                pe.wait_ge(max_ready, 1)
                nc.tensor.transpose(m_ps[0:1, 0:P], a_abs[:, 0:1], ident[:, :]).then_inc(row_done, 1)
            if k == 24:
                pe.wait_ge(scale_ready, 1)
                nc.tensor.matmul(m_ps[:, P:P + 1], ones[0:1, :], sc[0:1, 2:3], start=True, stop=True)\
                    .then_inc(bc_done, 1)
        gather_rest(0)
        prep_chunk(1)
        mlp(0)
        with pe.Fori(1, NC - 1) as c:
            chunk(c)
        pe.wait_ge(setup_done, 2)
        for k in range(EARLY, KT):
            gather_tile(NC - 1, k)
            if k in TR_H2_AT:
                transpose_h2(NC - 2, [TR_H2_AT.index(k)])
        gather_rest(NC - 1)

        def h2_there():
            pe.wait_ge(h2_copied, DH * NC)
            pe.wait_ge(v_stored, 32 * NC)

        return (lambda: mlp_up(NC - 1)), (lambda: mlp_down(NC - 1)), (lambda: transpose_h2(NC - 1)), h2_there

    return sync, pool, vector, scalar, tensor


def layer1(nc, mem, adj, x2_dram, out):
    sb, sem = mem.sb, mem.sem
    ident, ones = mem.ident, mem.ones
    h2t, v_hi, v_lo = mem.h2t, mem.v_hi, mem.v_lo
    a_sp, exp_scale, wvt = mem.a_sp, mem.exp_scale, mem.wvt
    KL = 4
    s_all = Cut(mem.big)([KT, CH], F32)
    cut = Cut(mem.small)
    t_q = cut([DH, 2, CH], F16)
    t_next = cut([DH, 2, CH], F16)
    p_32 = cut([X_RING, CH], F32)
    p_hi = cut([X_RING, CH], F16)
    p_lo = cut([X_RING, CH], F16)
    s_max = cut([CH], F32)
    max_diag = cut([TC, P], F32)
    t_32 = cut([CH], F32)
    max_b = cut([CH], F32)
    o_t = cut([TC, DH, P], F32)[:, :, :, :]
    assert cut.at <= mem.SMALL
    cut = Cut(mem.adj_pair[:, :, :].rearrange("p s n -> p (s n)"))
    adj_m = cut([2, KL, CH], U8)
    not_adj = cut([2, KL, CH], U8)
    x2_in, o_out, o_n = mem.rows_a, mem.rows_b, mem.rows_c
    exp_bias = sb("exp_bias", [P, 1], F32)
    max_col = sb("max_col", [P, TC], F32)
    r_sum = sb("r_sum", [P, TC, 2], F32)
    pv_ps = [mem.banks[:, i, :] for i in (0, 1, 4, 5)]
    qk_ps = [mem.banks[:, i, :] for i in (2, 3)]
    m_ps = [mem.banks[:, i, :] for i in (6, 7)]
    TAIL_PS = [m_ps[1], m_ps[0]] + qk_ps
    adj_loaded = [sem(f"adj_loaded{i}") for i in range(2)]
    bias_set = sem("bias_set")
    flipped, qk_done, masked, maxed = sem("flipped"), sem("qk_done"), sem("masked"), sem("maxed")
    t_done, t_rounded, t_split, t_copied, t_moved = sem("t_done"), sem("t_rounded"), sem("t_split"), sem("t_copied"), sem("t_moved")
    max_tr, max_red, max_dg, max_bc, max_ready = sem("max_tr"), sem("max_red"), sem("max_dg"), sem("max_bc"), sem("max_ready")
    shifted, exped, p_hi_done, p_lo_done, pv_done = sem("shifted"), sem("exped"), sem("p_hi_done"), sem("p_lo_done"), sem("pv_done")
    rs_chain, rs_ready, o_ready, o_tr, o_copied, proj_done = sem("rs_chain"), sem("rs_ready"), sem("o_ready"), sem("o_tr"), sem("o_copied"), sem("proj_done")
    out_ready, x2_loaded, out_stored = sem("out_ready"), sem("x2_loaded"), sem("out_stored")

    LOADS = KT // KL
    T_AT = [1, 7]
    TR_AT = [4, 8, 12, 16]
    PROJ_AT = [6, 10, 14, 18]
    LAST_TR_AT = [4, 11, 18, 25]
    LAST_PROJ_AT = [9, 16, 23, 30]

    def is0(c, n=0):
        return isinstance(c, int) and c <= n

    def sync(sp, finish):
        def load_adj(c, n, slot):
            if not (is0(c) and is0(n, 1)):
                sp.wait_ge(flipped, c * LOADS + n - 1)
            sp.dma_start(adj_m[:, slot, :, :], adj[bass.ds(n * (KL * P), KL * P), bass.ds(c * CH, CH)]
                         .rearrange("(k p) q -> p k q", p=P)).then_inc(adj_loaded[slot], 16)

        def load_chunk(c):
            with sp.Fori(0, LOADS // 2) as m:
                load_adj(c, m * 2, 0)
                load_adj(c, m * 2 + 1, 1)

        def load_x2(c):
            if not is0(c):
                sp.wait_ge(out_ready, TC * c)
            sp.dma_start(x2_in[:, :, :], x2_dram[bass.ds(c * CH, CH), :].rearrange("(t p) m -> p t m", p=P))\
                .then_inc(x2_loaded, 16)

        def store(c):
            sp.wait_ge(out_ready, TC * (c + 1))
            sp.dma_start(out[bass.ds(c * CH, CH), :].rearrange("(t p) m -> p t m", p=P), o_out[:, :, :])\
                .then_inc(out_stored, 16)

        adjacency_read, finish_rows, values_stored = finish
        adjacency_read()
        for n in range(LOADS):
            load_adj(0, n, n % 2)
            if n == 1:
                finish_rows()
            if n == 3:
                values_stored()
        load_x2(0)
        load_chunk(1)
        with sp.Fori(2, NC) as c:
            load_chunk(c)
            store(c - 2)
            load_x2(c - 1)
        store(NC - 2)
        load_x2(NC - 1)
        for t in range(TC):
            sp.wait_ge(out_ready, TC * (NC - 1) + t + 1)
            sp.dma_start(out[(NC - 1) * CH + t * P:(NC - 1) * CH + (t + 1) * P, :], o_out[:, t, :])\
                .then_inc(out_stored, 16)
        sp.wait_ge(out_stored, 16 * (NC - 1) + 16 * TC)

    def pool(pool):
        nc.gpsimd.memset(exp_bias[:, :], math.log(P_SCALE)).then_inc(bias_set, 1)

        def low(c, k):
            slot = k % X_RING
            pool.wait_ge(p_hi_done, KT * c + k + 1)
            if not (is0(c) and k < X_RING):
                pool.wait_ge(pv_done, KT * c + k - X_RING + 1)
            nc.gpsimd.tensor_tensor(p_lo[:, slot, :], p_32[:, slot, :], p_hi[:, slot, :], ALU.subtract)\
                .then_inc(p_lo_done, 1)

        for k in range(KT):
            low(0, k)
        with pool.Fori(1, NC) as c:
            for k in range(KT):
                low(c, k)

    def vector(dve, finish):
        rs_seq = Chain(dve, rs_chain, 1)

        def split_t(c, h):
            dve.wait_ge(t_rounded, DH * c + h + 1)
            nc.vector.tensor_tensor(t_next[:, h, 1, :], t_32[:, :], t_next[:, h, 0, :], ALU.subtract)\
                .then_inc(t_split, 1)

        def move_t(c):
            dve.wait_ge(t_split, DH * (c + 1))
            if not is0(c):
                dve.wait_ge(qk_done, KT * c)
            nc.vector.tensor_copy(t_q[:, :, :, :], t_next[:, :, :, :]).then_inc(t_moved, 1)

        def flip(c, n):
            dve.wait_ge(adj_loaded[n % 2], 16 * (LOADS // 2 * c + n // 2 + 1))
            if not (is0(c) and n < 2):
                dve.wait_ge(masked, KT * c + KL * (n - 1))
            nc.vector.tensor_single_scalar(
                not_adj[:, n % 2, :, :].rearrange("p k q -> p (k q)").bitcast(U32),
                adj_m[:, n % 2, :, :].rearrange("p k q -> p (k q)").bitcast(U32),
                0x01010101, ALU.bitwise_xor).then_inc(flipped, 1)

        def mask(c, k):
            if k % KL == 0:
                flip(c, k // KL)
                dve.wait_ge(flipped, LOADS * c + k // KL + 1)
            if not is0(c):
                dve.wait_ge(shifted, KT * (c - 1) + k + 1)
            dve.wait_ge(qk_done, KT * c + k + 1)
            nc.vector.scalar_tensor_tensor(s_all[:, k, :], not_adj[:, k // KL % 2, k % KL, :], NEG,
                                           qk_ps[k % QK_RING][:, :], ALU.mult, ALU.add).then_inc(masked, 1)

        def running_max(c, k):
            dve.wait_ge(masked, KT * c + k + 1)
            if not (is0(c) and k == 0):
                dve.wait_ge(maxed, KT * c + k)
            if k == 0:
                if not is0(c):
                    dve.wait_ge(max_tr, c)
                nc.vector.tensor_copy(s_max[:, :], s_all[:, 0, :]).then_inc(maxed, 1)
            else:
                nc.vector.tensor_tensor(s_max[:, :], s_max[:, :], s_all[:, k, :], ALU.max).then_inc(maxed, 1)

        def maxima(c):
            dve.wait_ge(max_tr, c + 1)
            nc.vector.tensor_reduce(out=max_col[:, :], in_=m_ps[0][:, :].rearrange("p (t k) -> p t k", t=TC),
                                    axis=AX.X, op=ALU.max).then_inc(max_red, 1)
            dve.wait_ge(max_red, 2 * c + 1)
            nc.vector.tensor_single_scalar(max_col[:, :], max_col[:, :], NEG_FLOOR, ALU.max).then_inc(max_red, 1)
            dve.wait_ge(max_red, 2 * c + 2)
            if not is0(c):
                dve.wait_ge(max_bc, c)
            for t in range(TC):
                nc.vector.tensor_scalar(max_diag[:, t, :], ident[:, :], max_col[:, t:t + 1], None, ALU.mult)\
                    .then_inc(max_dg, 1)

        def copy_max(c):
            dve.wait_ge(max_bc, c + 1)
            if not is0(c):
                dve.wait_ge(shifted, KT * c)
            nc.vector.tensor_copy(max_b[:, :], m_ps[0][:, :]).then_inc(max_ready, 1)
            dve.wait_ge(max_ready, c + 1)

        def shift(c, k):
            if not (is0(c) and k < X_RING):
                dve.wait_ge(p_lo_done, KT * c + k - X_RING + 1)
                dve.wait_ge(p_hi_done, KT * c + k - X_RING + 1)
            nc.vector.tensor_tensor(p_32[:, k % X_RING, :], s_all[:, k, :], max_b[:, :], ALU.subtract)\
                .then_inc(shifted, 1)

        def sums(c):
            dve.wait_ge(pv_done, KT * (c + 1))
            if not is0(c):
                dve.wait_ge(o_ready, TC * c)
            rs_seq.begin(c)
            for t in range(TC):
                last = nc.vector.tensor_single_scalar(r_sum[:, t, 0:1], pv_ps[t][:, D:D + 1], TINY, ALU.max)
            rs_seq.then(last)
            nc.vector.reciprocal(r_sum[:, :, 1], r_sum[:, :, 0]).then_inc(rs_ready, 1)
            rs_seq.end()

        def add_x2(c, t, bank=m_ps[1]):
            dve.wait_ge(proj_done, TC * c + t + 1)
            if t == 0:
                dve.wait_ge(x2_loaded, 16 * (c + 1))
                if not is0(c):
                    dve.wait_ge(out_stored, 16 * c)
            nc.vector.tensor_tensor(o_out[:, t, :], bank[:, D:2 * D], x2_in[:, t, :], ALU.add)\
                .then_inc(out_ready, 1)

        def chunk(c, first=False, more=True, more2=True):
            for k in range(AHEAD):
                shift(c, k)
            for k in range(KT):
                if more:
                    mask(c + 1, k)
                if k + AHEAD < KT:
                    shift(c, k + AHEAD)
                if more:
                    running_max(c + 1, k)
                if not first and k == 0:
                    sums(c - 1)
                if more2 and k - 2 in T_AT:
                    split_t(c + 2, T_AT.index(k - 2))
                proj_at = PROJ_AT if more else LAST_PROJ_AT
                if not first and k - 1 in proj_at:
                    add_x2(c - 1, proj_at.index(k - 1))
            if more2:
                move_t(c + 2)
            if more:
                maxima(c + 1)
                copy_max(c + 1)

        ln2_stats, ln2_scale = finish
        for h in range(DH):
            split_t(0, h)
        move_t(0)
        ln2_stats()
        for k in range(KT):
            mask(0, k)
            if k == 2:
                ln2_scale()
            if k >= 1:
                running_max(0, k - 1)
            if k - 2 in T_AT:
                split_t(1, T_AT.index(k - 2))
        move_t(1)
        running_max(0, KT - 1)
        maxima(0)
        copy_max(0)
        chunk(0, first=True)
        with dve.Fori(1, NC - 2) as c:
            chunk(c)
        chunk(NC - 2, more2=False)
        chunk(NC - 1, more=False, more2=False)
        sums(NC - 1)
        for t in range(TC):
            add_x2(NC - 1, t, TAIL_PS[t])

    def scalar(act, finish):
        def round_t(c, h):
            act.wait_ge(t_done, DH * c + h + 1)
            if not (is0(c) and h == 0):
                act.wait_ge(t_split, DH * c + h)
            nc.scalar.activation(t_32[:, :], m_ps[0][:, :], ACT.Copy, scale=1.0 / H_SCALE)\
                .then_inc(t_copied, 1)
            act.wait_ge(t_copied, DH * c + h + 1)
            if not is0(c) and h == 0:
                act.wait_ge(t_moved, c)
            nc.scalar.activation(t_next[:, h, 0, :], t_32[:, :], ACT.Copy).then_inc(t_rounded, 1)

        def exps(c, k):
            act.wait_ge(shifted, KT * c + k + 1)
            slot = k % X_RING
            nc.scalar.activation(p_32[:, slot, :], p_32[:, slot, :], ACT.Exp, bias=exp_bias[:, :],
                                 scale=exp_scale[:, :])\
                .then_inc(exped, 1)
            act.wait_ge(exped, KT * c + k + 1)
            if not (is0(c) and k < X_RING):
                act.wait_ge(pv_done, KT * c + k - X_RING + 1)
            nc.scalar.activation(p_hi[:, slot, :], p_32[:, slot, :], ACT.Copy)\
                .then_inc(p_hi_done, 1)

        def evacuate(c):
            act.wait_ge(rs_ready, c + 1)
            if not is0(c):
                act.wait_ge(o_tr, TC * c)
            for t in range(TC):
                nc.scalar.activation(o_n[:, t, :], pv_ps[t][:, 0:D], ACT.Copy, scale=r_sum[:, t, 1:2])\
                    .then_inc(o_ready, 1)

        def copy_ot(c, t, bank=m_ps[1]):
            act.wait_ge(o_tr, TC * c + t + 1)
            if bank is m_ps[1] and not (is0(c) and t == 0):
                act.wait_ge(proj_done, TC * c + t)
            nc.scalar.activation(o_t[:, t, :, :], bank[:, 0:D].rearrange("p (h q) -> p h q", h=DH), ACT.Copy)\
                .then_inc(o_copied, 1)

        def chunk(c, first=False, more=True, more2=True):
            tr_at = TR_AT if more else LAST_TR_AT
            for k in range(KT):
                exps(c, k)
                if not first and k == 0:
                    evacuate(c - 1)
                if more2 and k - 1 in T_AT:
                    round_t(c + 2, T_AT.index(k - 1))
                if not first and k - 1 in tr_at:
                    copy_ot(c - 1, tr_at.index(k - 1))

        mlp_relu, ln2_std, ln2_rows, copy_h2t = finish
        round_t(0, 0)
        mlp_relu()
        round_t(0, 1)
        round_t(1, 0)
        ln2_std()
        round_t(1, 1)
        ln2_rows()
        copy_h2t()
        act.wait_ge(bias_set, 1)
        chunk(0, first=True)
        with act.Fori(1, NC - 2) as c:
            chunk(c)
        chunk(NC - 2, more2=False)
        chunk(NC - 1, more=False, more2=False)
        evacuate(NC - 1)
        for t in range(TC):
            copy_ot(NC - 1, t, TAIL_PS[t])

    def tensor(pe, finish):
        def t_product(c, h):
            if not (is0(c) and h == 0):
                pe.wait_ge(t_copied, DH * c + h)
            if not is0(c, 1):
                pe.wait_ge(max_ready, c - 1)
            n = 0
            for o in range(DH):
                for s, u in ((0, 0), (0, 1), (1, 0)):
                    last = nc.tensor.matmul(m_ps[0][:, :], a_sp[:, o, s, h * P:(h + 1) * P],
                                            h2t[:, o, u, bass.ds(c * CH, CH)], start=(n == 0), stop=(n == 5))
                    n += 1
            last.then_inc(t_done, 1)

        def scores(c, k):
            if k == 0:
                pe.wait_ge(t_moved, c + 1)
            if not (is0(c) and k < QK_RING):
                pe.wait_ge(masked, KT * c + k - QK_RING + 1)
            n = 0
            for h in range(DH):
                for s, u in ((0, 0), (0, 1), (1, 0)):
                    last = nc.tensor.matmul(qk_ps[k % QK_RING][:, :], h2t[:, h, s, k * P:(k + 1) * P],
                                            t_q[:, h, u, :], start=(n == 0), stop=(n == 5))
                    n += 1
            last.then_inc(qk_done, 1)

        def values(c, k):
            pe.wait_ge(p_lo_done, KT * c + k + 1)
            if k == 0 and not is0(c):
                pe.wait_ge(o_ready, TC * c)
            slot = k % X_RING
            for t in range(TC):
                q = slice(t * P, (t + 1) * P)
                nc.tensor.matmul(pv_ps[t][:, 0:D + 1], p_hi[:, slot, q], v_hi[:, k, 0:D + 1],
                                 start=(k == 0), stop=False)
                nc.tensor.matmul(pv_ps[t][:, 0:D], p_hi[:, slot, q], v_lo[:, k, :], start=False, stop=False,
                                 skip_group_check=True)
                last = nc.tensor.matmul(pv_ps[t][:, 0:D + 1], p_lo[:, slot, q], v_hi[:, k, 0:D + 1],
                                        start=False, stop=(k == KT - 1))
            last.then_inc(pv_done, 1)

        def transpose_max(c):
            pe.wait_ge(maxed, KT * (c + 1))
            if not (isinstance(c, int) and c == NC - 1):
                pe.wait_ge(t_copied, DH * (c + 2))
            for t in range(TC):
                last = nc.tensor.transpose(m_ps[0][:, t * P:(t + 1) * P], s_max[:, t * P:(t + 1) * P], ident[:, :])
            last.then_inc(max_tr, 1)

        def spread_max(c):
            pe.wait_ge(max_dg, TC * (c + 1))
            for t in range(TC):
                last = nc.tensor.matmul(m_ps[0][:, t * P:(t + 1) * P], ones[:, :], max_diag[:, t, :],
                                        start=True, stop=True)
            last.then_inc(max_bc, 1)

        def transpose_o(c, t, bank=m_ps[1]):
            pe.wait_ge(o_ready, TC * c + t + 1)
            if bank is m_ps[1] and not (is0(c) and t == 0):
                pe.wait_ge(out_ready, TC * c + t)
            for h in range(DH):
                last = nc.tensor.transpose(bank[:, h * P:(h + 1) * P], o_n[:, t, h * P:(h + 1) * P], ident[:, :])
            last.then_inc(o_tr, 1)

        def project(c, t, bank=m_ps[1]):
            pe.wait_ge(o_copied, TC * c + t + 1)
            for h in range(DH):
                last = nc.tensor.matmul(bank[:, D:2 * D], o_t[:, t, h, :], wvt[:, h, :],
                                        start=(h == 0), stop=(h == DH - 1))
            last.then_inc(proj_done, 1)

        def chunk(c, first=False, more=True, more2=True):
            for k in range(KT):
                if more and not (first and k < 2):
                    scores(c + 1, k)
                if more2 and k in T_AT:
                    t_product(c + 2, T_AT.index(k))
                if k >= LAG:
                    values(c, k - LAG)
                tr_at, proj_at = (TR_AT, PROJ_AT) if more else (LAST_TR_AT, LAST_PROJ_AT)
                if not first and k in tr_at:
                    transpose_o(c - 1, tr_at.index(k))
                if not first and k in proj_at:
                    project(c - 1, proj_at.index(k))
            for k in range(KT - LAG, KT):
                if more and k == KT - LAG + 1:
                    transpose_max(c + 1)
                if more and k == KT - LAG + 3:
                    spread_max(c + 1)
                values(c, k)

        mlp_up, mlp_down, transpose_h2, h2_there = finish
        t_product(0, 0)
        mlp_up()
        t_product(0, 1)
        mlp_down()
        for k in range(KT):
            if k == KT - TC:
                h2_there()
            scores(0, k)
            if k in T_AT:
                t_product(1, T_AT.index(k))
            if k == 12:
                transpose_h2()
        scores(1, 0)
        transpose_max(0)
        scores(1, 1)
        spread_max(0)
        chunk(0, first=True)
        with pe.Fori(1, NC - 2) as c:
            chunk(c)
        chunk(NC - 2, more2=False)
        chunk(NC - 1, more=False, more2=False)
        transpose_o(NC - 1, 0, TAIL_PS[0])
        for t in range(TC):
            if t + 1 < TC:
                transpose_o(NC - 1, t + 1, TAIL_PS[t + 1])
            project(NC - 1, t, TAIL_PS[t])

    return sync, pool, vector, scalar, tensor


_INS = ["x", "adj", "L0_gnn_W1", "L0_gnn_b1", "L0_gnn_W2", "L0_gnn_b2", "L1_gnn_Wq", "L1_gnn_Wk", "L1_gnn_Wv"]


def kernel(**inputs):
    import numpy as _np
    import concourse.bacc as _bacc
    from concourse import mybir as _mybir
    from concourse.bass_utils import run_bass_kernel_spmd as _run

    nc = _bacc.Bacc("TRN2", target_bir_lowering=False, num_devices=1)
    arrays, args = {}, []
    for name in _INS:
        a = _np.ascontiguousarray(inputs[name])
        if a.dtype == _np.bool_:
            a = a.view(_np.uint32)
        arrays[f"in_{name}"] = a
        args.append(nc.dram_tensor(f"in_{name}", a.shape, _mybir.dt.from_np(a.dtype), kind="ExternalInput").ap())
    out = nc.dram_tensor("out_x", (4096, 256), _mybir.dt.float32, kind="ExternalOutput").ap()
    args[1] = args[1].bitcast(_mybir.dt.uint8)
    build(nc, *args, out)
    r = _run(nc, [arrays], core_ids=[0])
    return r.results[0]["out_x"]
```
